# Optimizing a Trainium2 kernel written in Bass

```python
import numpy as np
import jax
import jax.numpy as jnp

def _softmax(x, axis=-1):
    return jax.nn.softmax(x, axis=axis)

def _gelu(x):
    return jax.nn.gelu(x, approximate=True)

def _silu(x):
    return jax.nn.silu(x)

def _sigmoid(x):
    return jax.nn.sigmoid(x)

def _layernorm(x, axis=-1, eps=1e-05):
    m = jnp.mean(x, axis=axis, keepdims=True)
    v = jnp.var(x, axis=axis, keepdims=True)
    return (x - m) / jnp.sqrt(v + eps)

def _scatter_add(tgt, idx, src, axis=0):
    return tgt.at[idx].add(src)

def _segment_sum(src, seg, n):
    return jax.ops.segment_sum(src, seg, n)
kernel_name = 'mk_seq_preln_d2_jaxref_r8_7f4aa4'

def setup_inputs(seed: int=0):
    np.random.seed(seed)
    _w = jnp.asarray

    def _L0_attn_setup():
        import math
        import jax, jax.numpy as jnp
        import numpy as np
        HIDDEN = 128
        NUM_HEADS = 16
        NUM_QUERIES = 2
        NUM_Q_HEADS = NUM_HEADS * NUM_QUERIES
        HEAD_DIM = 64
        Q_DIM = NUM_Q_HEADS * HEAD_DIM
        KV_DIM = NUM_HEADS * HEAD_DIM
        BATCH, SEQ = (4, 128)

        def _alibi_slopes(num_heads: int) -> np.ndarray:
            closest_pow2 = 2 ** int(math.floor(math.log2(num_heads)))
            base = 2.0 ** (-2.0 ** (-(math.log2(closest_pow2) - 3)))
            powers = np.arange(1, closest_pow2 + 1, dtype=np.float32)
            slopes = base ** powers
            if closest_pow2 != num_heads:
                extra_base = 2.0 ** (-2.0 ** (-(math.log2(2 * closest_pow2) - 3)))
                extra_powers = np.arange(1, 2 * (num_heads - closest_pow2) + 1, 2, dtype=np.float32)
                slopes = np.concatenate([slopes, extra_base ** extra_powers])
            return slopes[:num_heads].astype(np.float32)
        ALIBI_SLOPES = jnp.asarray(_alibi_slopes(NUM_Q_HEADS))
        key = jax.random.key(seed)
        k1, k2, k3 = jax.random.split(key, 3)
        inputs = jax.random.normal(k1, (BATCH, SEQ, HIDDEN), dtype=jnp.float32)
        W_qkv = jax.random.normal(k2, (HIDDEN, Q_DIM + 2 * KV_DIM), dtype=jnp.float32) * (1.0 / math.sqrt(HIDDEN))
        W_out = jax.random.normal(k3, (Q_DIM, HIDDEN), dtype=jnp.float32) * (1.0 / math.sqrt(Q_DIM))
        return {'inputs': inputs, 'W_qkv': W_qkv, 'W_out': W_out}
    _L0_attn_in = _L0_attn_setup()

    def _L0_ffn_setup():
        import jax, jax.numpy as jnp
        import numpy as np
        DIM = 128
        HIDDEN = 384
        SCALE = 1.0 / 127.0

        def _dequant(w_int, dtype):
            return w_int.astype(dtype) * jnp.asarray(SCALE, dtype)
        key = jax.random.key(seed)
        k_x, k_g, k_u, k_d = jax.random.split(key, 4)
        x = jax.random.normal(k_x, (4, 256, DIM), dtype=jnp.float32)
        w_gate = jax.random.randint(k_g, (HIDDEN, DIM), -127, 128, dtype=jnp.int32)
        w_up = jax.random.randint(k_u, (HIDDEN, DIM), -127, 128, dtype=jnp.int32)
        w_down = jax.random.randint(k_d, (DIM, HIDDEN), -127, 128, dtype=jnp.int32)
        return {'x': x, 'w_gate': w_gate, 'w_up': w_up, 'w_down': w_down}
    _L0_ffn_in = _L0_ffn_setup()

    def _L1_attn_setup():
        import jax, jax.numpy as jnp
        import numpy as np
        DIM = 128
        HEADS = 16
        HEAD_DIM = 64
        key = jax.random.key(seed)
        ks = jax.random.split(key, 6)
        inner = HEADS * HEAD_DIM
        s = 0.02
        return {'x': jax.random.normal(ks[0], (2, 256, DIM), dtype=jnp.float32), 'Wq': jax.random.normal(ks[1], (DIM, inner), dtype=jnp.float32) * s, 'Wk': jax.random.normal(ks[2], (DIM, inner), dtype=jnp.float32) * s, 'Wv': jax.random.normal(ks[3], (DIM, inner), dtype=jnp.float32) * s, 'Wo': jax.random.normal(ks[4], (inner, DIM), dtype=jnp.float32) * s, 'bo': jax.random.normal(ks[5], (DIM,), dtype=jnp.float32) * s}
    _L1_attn_in = _L1_attn_setup()

    def _L1_ffn_setup():
        import jax, jax.numpy as jnp
        import numpy as np
        CAPACITY_FACTOR = 1.25
        key = jax.random.key(seed)
        ks = jax.random.split(key, 6)
        B, S, H, E = (4, 512, 128, 8)
        scale = 1.0 / np.sqrt(H)
        return {'tokens': jax.random.normal(ks[0], (B, S, H), dtype=jnp.float32), 'gate_w': jax.random.normal(ks[1], (E, H), dtype=jnp.float32) * scale, 'w1': jax.random.normal(ks[2], (E, H, H), dtype=jnp.float32) * scale, 'b1': jax.random.normal(ks[3], (E, H), dtype=jnp.float32) * 0.01, 'w2': jax.random.normal(ks[4], (E, H, H), dtype=jnp.float32) * scale, 'b2': jax.random.normal(ks[5], (E, H), dtype=jnp.float32) * 0.01}
    _L1_ffn_in = _L1_ffn_setup()
    _d = {'L0_attn_inputs': _L0_attn_in['inputs'], 'L0_attn_W_qkv': _L0_attn_in['W_qkv'], 'L0_attn_W_out': _L0_attn_in['W_out'], 'L0_ffn_w_gate': _L0_ffn_in['w_gate'], 'L0_ffn_w_up': _L0_ffn_in['w_up'], 'L0_ffn_w_down': _L0_ffn_in['w_down'], 'L1_attn_Wq': _L1_attn_in['Wq'], 'L1_attn_Wk': _L1_attn_in['Wk'], 'L1_attn_Wv': _L1_attn_in['Wv'], 'L1_attn_Wo': _L1_attn_in['Wo'], 'L1_attn_bo': _L1_attn_in['bo'], 'L1_ffn_gate_w': _L1_ffn_in['gate_w'], 'L1_ffn_w1': _L1_ffn_in['w1'], 'L1_ffn_b1': _L1_ffn_in['b1'], 'L1_ffn_w2': _L1_ffn_in['w2'], 'L1_ffn_b2': _L1_ffn_in['b2']}
    _x0 = _d['L0_attn_inputs']
    _d['L0_attn_inputs'] = jax.random.normal(jax.random.fold_in(jax.random.key(seed), 1), (2, 1024, 128), dtype=_x0.dtype)
    del _x0
    return _d

def reference(L0_attn_inputs, L0_attn_W_qkv, L0_attn_W_out, L0_ffn_w_gate, L0_ffn_w_up, L0_ffn_w_down, L1_attn_Wq, L1_attn_Wk, L1_attn_Wv, L1_attn_Wo, L1_attn_bo, L1_ffn_gate_w, L1_ffn_w1, L1_ffn_b1, L1_ffn_w2, L1_ffn_b2):

    def _L0_attn_ref(inputs, W_qkv, W_out):
        import math
        import jax, jax.numpy as jnp
        import numpy as np
        HIDDEN = 128
        NUM_HEADS = 16
        NUM_QUERIES = 2
        NUM_Q_HEADS = NUM_HEADS * NUM_QUERIES
        HEAD_DIM = 64
        Q_DIM = NUM_Q_HEADS * HEAD_DIM
        KV_DIM = NUM_HEADS * HEAD_DIM
        BATCH, SEQ = (4, 128)

        def _alibi_slopes(num_heads: int) -> np.ndarray:
            closest_pow2 = 2 ** int(math.floor(math.log2(num_heads)))
            base = 2.0 ** (-2.0 ** (-(math.log2(closest_pow2) - 3)))
            powers = np.arange(1, closest_pow2 + 1, dtype=np.float32)
            slopes = base ** powers
            if closest_pow2 != num_heads:
                extra_base = 2.0 ** (-2.0 ** (-(math.log2(2 * closest_pow2) - 3)))
                extra_powers = np.arange(1, 2 * (num_heads - closest_pow2) + 1, 2, dtype=np.float32)
                slopes = np.concatenate([slopes, extra_base ** extra_powers])
            return slopes[:num_heads].astype(np.float32)
        ALIBI_SLOPES = jnp.asarray(_alibi_slopes(NUM_Q_HEADS))
        B, S, _ = inputs.shape
        qkv = inputs @ W_qkv
        q = qkv[..., :Q_DIM].reshape(B, S, NUM_Q_HEADS, HEAD_DIM).transpose(0, 2, 1, 3)
        k = qkv[..., Q_DIM:Q_DIM + KV_DIM].reshape(B, S, NUM_HEADS, HEAD_DIM).transpose(0, 2, 1, 3)
        v = qkv[..., Q_DIM + KV_DIM:].reshape(B, S, NUM_HEADS, HEAD_DIM).transpose(0, 2, 1, 3)
        k = jnp.repeat(k, NUM_QUERIES, axis=1)
        v = jnp.repeat(v, NUM_QUERIES, axis=1)
        pos = jnp.arange(S)
        rel = (pos[None, :] - pos[:, None]).astype(jnp.float32)
        bias = ALIBI_SLOPES[:, None, None] * rel[None, :, :]
        scores = jnp.einsum('bhqd,bhkd->bhqk', q, k) / math.sqrt(HEAD_DIM)
        scores = scores + bias[None]
        causal = pos[:, None] >= pos[None, :]
        scores = jnp.where(causal[None, None], scores, -jnp.inf)
        attn = jax.nn.softmax(scores, axis=-1)
        out = jnp.einsum('bhqk,bhkd->bhqd', attn, v)
        out = out.transpose(0, 2, 1, 3).reshape(B, S, Q_DIM)
        return out @ W_out

    def _L0_ffn_ref(x, w_gate, w_up, w_down):
        import jax, jax.numpy as jnp
        import numpy as np
        DIM = 128
        HIDDEN = 384
        SCALE = 1.0 / 127.0

        def _dequant(w_int, dtype):
            return w_int.astype(dtype) * jnp.asarray(SCALE, dtype)
        wg = _dequant(w_gate, x.dtype)
        wu = _dequant(w_up, x.dtype)
        wd = _dequant(w_down, x.dtype)
        gate = jnp.einsum('bsd,hd->bsh', x, wg)
        up = jnp.einsum('bsd,hd->bsh', x, wu)
        h = jax.nn.silu(gate) * up
        return jnp.einsum('bsh,dh->bsd', h, wd)

    def _L1_attn_ref(x, Wq, Wk, Wv, Wo, bo):
        import jax, jax.numpy as jnp
        import numpy as np
        DIM = 128
        HEADS = 16
        HEAD_DIM = 64
        N, S, _ = x.shape
        scale = 1.0 / np.sqrt(HEAD_DIM).astype(np.float32)
        q = (x @ Wq).reshape(N, S, HEADS, HEAD_DIM).transpose(0, 2, 1, 3)
        k = (x @ Wk).reshape(N, S, HEADS, HEAD_DIM).transpose(0, 2, 1, 3)
        v = (x @ Wv).reshape(N, S, HEADS, HEAD_DIM).transpose(0, 2, 1, 3)
        logits = jnp.einsum('nhid,nhjd->nhij', q, k) * scale
        causal = 1000000000.0 * (jnp.tril(jnp.ones((S, S), dtype=logits.dtype)) - 1.0)
        logits = logits + causal[None, None, :, :]
        attn = jax.nn.softmax(logits, axis=-1)
        out = jnp.einsum('nhij,nhjd->nhid', attn, v)
        out = out.transpose(0, 2, 1, 3).reshape(N, S, HEADS * HEAD_DIM)
        return out @ Wo + bo

    def _L1_ffn_ref(tokens, gate_w, w1, b1, w2, b2):
        import jax, jax.numpy as jnp
        import numpy as np
        CAPACITY_FACTOR = 1.25
        B, S, H = tokens.shape
        E = gate_w.shape[0]
        N = B * S
        cap = int(CAPACITY_FACTOR * N / E)
        x = tokens.reshape(N, H)
        probs = jax.nn.softmax(x @ gate_w.T, axis=-1)
        top2_w, top2_idx = jax.lax.top_k(probs, 2)
        a_e = top2_idx.reshape(-1)
        a_w = top2_w.reshape(-1)
        tok_id = jnp.arange(2 * N) // 2
        counts = jnp.bincount(a_e, length=E)
        keep = counts <= cap
        valid = keep[a_e]
        onehot = jax.nn.one_hot(a_e, E, dtype=jnp.int32)
        pos = jnp.take_along_axis(jnp.cumsum(onehot, axis=0) - 1, a_e[:, None], axis=1)[:, 0]
        p = jnp.where(valid, jnp.minimum(pos, cap - 1), cap)
        x_a = x[tok_id]
        buf = jnp.zeros((E, cap + 1, H), dtype=x.dtype).at[a_e, p].set(x_a)
        h = jax.nn.silu(jnp.einsum('ech,efh->ecf', buf, w1) + b1[:, None, :])
        y = jnp.einsum('ecf,egf->ecg', h, w2) + b2[:, None, :]
        contrib = y[a_e, p] * (a_w * valid.astype(x.dtype))[:, None]
        out = contrib.reshape(N, 2, H).sum(axis=1)
        return out.reshape(B, S, H)
    x = L0_attn_inputs
    x = x + _L0_attn_ref(_layernorm(x, axis=-1), L0_attn_W_qkv, L0_attn_W_out)
    x = x + _L0_ffn_ref(_layernorm(x, axis=-1), L0_ffn_w_gate, L0_ffn_w_up, L0_ffn_w_down)
    x = x + _L1_attn_ref(_layernorm(x, axis=-1), L1_attn_Wq, L1_attn_Wk, L1_attn_Wv, L1_attn_Wo, L1_attn_bo)
    x = x + _L1_ffn_ref(_layernorm(x, axis=-1), L1_ffn_gate_w, L1_ffn_w1, L1_ffn_b1, L1_ffn_w2, L1_ffn_b2)
    return x

_drawn_inputs = setup_inputs


def setup_inputs(seed=0):
    import zlib

    import numpy as np

    out = dict(_drawn_inputs(seed))
    spreads = {}
    factors = {'L1_attn_Wq': 32.754,
     'L1_attn_Wk': 32.809,
     'L1_attn_Wv': 32.09,
     'L1_attn_Wo': 31.902,
     'L1_attn_bo': 64.0}
    for name, (base, spread) in spreads.items():
        noise = np.random.default_rng([zlib.crc32(name.encode()), seed]).standard_normal(out[name].shape)
        drawn = base * np.exp(spread * noise) if base else spread * noise
        out[name] = jnp.asarray(drawn.astype(out[name].dtype))
    for name, factor in factors.items():
        out[name] = (out[name] * factor).astype(out[name].dtype)
    return out
```

```python
import numpy as np
import concourse.bass as bass
from concourse import mybir
from contextlib import ExitStack

F32 = mybir.dt.float32
F32R = mybir.dt.float32r
I32 = mybir.dt.int32
ALU = mybir.AluOpType
ACT = mybir.ActivationFunctionType
AX = mybir.AxisListType

P = 128
C = 128
BATCH = 2
SEQ = 1024
TOK = BATCH * SEQ
NT = TOK // P
QT = SEQ // P
D = 64
KVH = 16
FH = 384
E = 8
CAP = int(1.25 * TOK / E)
EPS = 1e-5
MASKED = -1e34
LANES = 4


def alibi_slopes(n):
    base = 2.0 ** (-2.0 ** (-(np.log2(n) - 3)))
    return (base ** np.arange(1, n + 1, dtype=np.float32)).astype(np.float32)


class Core:

    def __init__(self, nc, ctx):
        self.nc = nc

        def sb(name, shape, dt=F32):
            return ctx.enter_context(nc.sbuf_tensor(name, shape, dt))

        def ps(name, cols):
            return ctx.enter_context(nc.psum_tensor(name, [P, cols], F32))

        self.x = sb("x", [P, NT, C])
        self.ident = sb("ident", [P, P])
        self.ones_row = sb("ones_row", [1, P])
        self.S = [ps("S0", 1024), ps("S1", 1024)]
        self.TP = [ps("TP0", 512), ps("TP1", 512)]
        self.O = ps("O", 512)
        self.PJ = ps("PJ", 512)


def wait_apart(eng, sem, value, passed):
    wait(eng, sem, value)
    if not isinstance(value, int):
        eng.sem_inc(passed, 1)


def wait(eng, sem, value):
    if isinstance(value, int) and value <= 0:
        return
    eng.wait_ge(sem, value)


class Norm:

    def __init__(self, core, ctx, name, exact):
        nc = core.nc
        self.core, self.exact = core, exact

        def sb(n, shape, dt=F32):
            return ctx.enter_context(nc.sbuf_tensor(f"{name}_{n}", shape, dt))

        def sem(n):
            return ctx.enter_context(nc.semaphore(f"{name}_{n}"))

        self.xn = sb("xn", [P, NT, C])
        self.sq = sb("sq", [P, LANES, C])
        self.mean = sb("mean", [P, NT])
        self.var = sb("var", [P, NT])
        self.std = sb("std", [P, NT])
        self.rstd = sb("rstd", [P, NT])
        self.tmp = sb("tmp", [P, NT])
        if exact:
            self.xT = sb("xT", [P, TOK])
        self.dve_done = sem("dve_done")
        self.var_ready = sem("var_ready")
        self.std_ready = sem("std_ready")
        self.xn_ready = sem("xn_ready")
        self.turned = sem("turned")
        self.rounded = sem("rounded")
        self.split = sem("split")

    STEPS = NT // LANES

    def vector(self, dve, hi=None, lo=None):
        nc, x = self.core.nc, self.core.x
        n = [0]

        def then(ins):
            n[0] += 1
            ins.then_inc(self.dve_done, 1)
            dve.wait_ge(self.dve_done, n[0])

        def wide(ap):
            return ap.unsqueeze(2).broadcast_to([P, LANES, C])

        for g in range(self.STEPS):
            s = slice(g * LANES, (g + 1) * LANES)
            then(nc.vector.reduce_sum(self.mean[:, s], x[:, s, :], axis=AX.X))
            then(nc.vector.tensor_scalar(self.mean[:, s], self.mean[:, s], 1.0 / C, None, ALU.mult))
            then(nc.vector.tensor_tensor(self.xn[:, s, :], x[:, s, :], wide(self.mean[:, s]), ALU.subtract))
            then(nc.vector.tensor_tensor(self.sq[:], self.xn[:, s, :], self.xn[:, s, :], ALU.mult))
            then(nc.vector.reduce_sum(self.var[:, s], self.sq[:], axis=AX.X))
            nc.vector.tensor_scalar(self.var[:, s], self.var[:, s], 1.0 / C, EPS, ALU.mult, ALU.add)\
                .then_inc(self.var_ready, 1)
        for g in range(self.STEPS):
            s = slice(g * LANES, (g + 1) * LANES)
            dve.wait_ge(self.std_ready, g + 1)
            then(nc.vector.reciprocal(self.rstd[:, s], self.std[:, s]))
            then(nc.vector.tensor_tensor(self.tmp[:, s], self.rstd[:, s], self.rstd[:, s], ALU.mult))
            then(nc.vector.tensor_tensor(self.tmp[:, s], self.tmp[:, s], self.var[:, s], ALU.mult))
            then(nc.vector.tensor_scalar(self.tmp[:, s], self.tmp[:, s], -0.5, 1.5, ALU.mult, ALU.add))
            then(nc.vector.tensor_tensor(self.rstd[:, s], self.rstd[:, s], self.tmp[:, s], ALU.mult))
            nc.vector.tensor_tensor(self.xn[:, s, :], self.xn[:, s, :], wide(self.rstd[:, s]), ALU.mult)\
                .then_inc(self.xn_ready, 1)
        if not self.exact:
            for g in range(self.STEPS):
                cols = slice(g * 512, (g + 1) * 512)
                dve.wait_ge(self.rounded, g + 1)
                nc.vector.tensor_tensor(lo[:, cols], self.core.TP[g % 2][:], hi[:, cols].bitcast(F32),
                                        ALU.subtract).then_inc(self.split, 1)

    def scalar(self, act, hi=None):
        nc = self.core.nc
        for g in range(self.STEPS):
            s = slice(g * LANES, (g + 1) * LANES)
            act.wait_ge(self.var_ready, g + 1)
            nc.scalar.activation(self.std[:, s], self.var[:, s], ACT.Sqrt).then_inc(self.std_ready, 1)
        for g in range(self.STEPS):
            act.wait_ge(self.turned, g + 1)
            out = self.xT if self.exact else hi
            nc.scalar.activation(out[:, g * 512:(g + 1) * 512], self.core.TP[g % 2][:], ACT.Copy)\
                .then_inc(self.rounded, 1)

    def tensor(self, pe):
        nc = self.core.nc
        for g in range(self.STEPS):
            pe.wait_ge(self.xn_ready, g + 1)
            if g >= 2:
                pe.wait_ge(self.rounded if self.exact else self.split, g - 1)
            for n in range(LANES):
                last = nc.tensor.transpose(self.core.TP[g % 2][:, n * P:(n + 1) * P],
                                           self.xn[:, g * LANES + n, :], self.core.ident[:])
            last.then_inc(self.turned, 1)


class Attention:

    def __init__(self, core, ctx, name, nq, w_q, w_k, w_out, slopes):
        nc = core.nc
        self.core, self.nq, self.name = core, nq, name
        self.w_q, self.w_k, self.w_out = w_q, w_k, w_out
        self.alibi = slopes is not None
        self.n = 2 * nq * QT
        self.groups = self.n // 4
        self.chunks = 12 * self.n // QT
        self.parts = 1 + nq
        self.proj = 2 * self.parts

        def sb(n, shape, dt=F32):
            return ctx.enter_context(nc.sbuf_tensor(f"{name}_{n}", shape, dt))

        def sem(n):
            return ctx.enter_context(nc.semaphore(f"{name}_{n}"))

        self.xh = sb("xh", [P, TOK], F32R)
        self.xl = sb("xl", [P, TOK], F32R)
        self.V = sb("V", [P, NT, KVH * D])
        if self.alibi:
            self.rel = sb("rel", [P, SEQ])
            self.slopes = sb("slopes", [P, nq * KVH])
            self.slope = sb("slope", [P, nq])
        self.bias = [sb(f"bias{h}", [P, SEQ]) for h in range(nq if self.alibi else 1)]

    def loop_memory(self, ctx):
        nc, name, nq = self.core.nc, self.name, self.nq

        def sb(n, shape, dt=F32):
            return ctx.enter_context(nc.sbuf_tensor(f"{name}_{n}", shape, dt))

        def sem(n):
            return ctx.enter_context(nc.semaphore(f"{name}_{n}"))

        self.raw_qk = sb("raw_qk", [P, self.parts, D])
        self.raw_out = sb("raw_out", [P, nq, C])
        self.w_proj = sb("w_proj", [P, self.parts, 2, 2, D], F32R)
        self.w_o = sb("w_o", [P, nq, C])
        self.KH = [sb(f"KH{b}", [P, SEQ], F32R) for b in range(2)]
        self.KL = [sb(f"KL{b}", [P, SEQ], F32R) for b in range(2)]
        self.Q = [[sb(f"Q{b}{h}", [P, SEQ], F32R) for h in range(nq)] for b in range(2)]
        self.VS = [sb(f"VS{b}", [P, QT, 2, D], F32R) for b in range(2)]
        self.prob = [sb(f"prob{i}", [P, SEQ]) for i in range(4)]
        self.neg_max = sb("neg_max", [P, 4])
        self.row_sum = sb("row_sum", [P, 16])
        self.recip = sb("recip", [P, 16])
        self.PH = [sb(f"PH{g}", [P, 4 * (g + 1), 512], F32R) for g in range(2)]
        self.PL = [sb(f"PL{g}", [P, 4 * (g + 1), 512], F32R) for g in range(2)]
        self.o_sb = [sb(f"o_sb{i}", [P, 512]) for i in range(2)]

        self.qk_loaded = sem("qk_loaded")
        self.out_loaded = sem("out_loaded")
        self.w_hi = sem("w_hi")
        self.w_lo = sem("w_lo")
        self.w_o_ready = sem("w_o_ready")
        self.v_hi = sem("v_hi")
        self.v_lo = sem("v_lo")
        self.bias_ready = sem("bias_ready")
        self.slope_ready = sem("slope_ready")
        self.passed = sem("passed")
        self.pool_passed = sem("pool_passed")
        self.pj_done = sem("pj_done")
        self.pj_hi = sem("pj_hi")
        self.pj_lo = sem("pj_lo")
        self.scored = sem("scored")
        self.maxed = sem("maxed")
        self.exped = sem("exped")
        self.turned = sem("turned")
        self.p_hi = sem("p_hi")
        self.p_lo = sem("p_lo")
        self.valued = sem("valued")
        self.o_copied = sem("o_copied")
        self.out_done = sem("out_done")
        self.recip_done = sem("recip_done")
        self.added = sem("added")

    def place(self, s):
        s %= self.n
        return s // (self.nq * QT), (s // QT) % self.nq, s % QT

    def first_chunk(self, s):
        t = s % QT
        return (s // QT) * 12 + (t if t < 4 else 4 + 2 * (t - 4))

    def end_chunk(self, s):
        return self.first_chunk(s) + (1 if s % QT < 4 else 2)

    def at(self, i, per_turn, count):
        return i * per_turn + count

    def projections(self, s, last):
        half = self.n // 2
        phase, k = s // half, s % half
        if s >= self.n or (phase == 1 and last):
            return None
        at = [1 + 2 * m for m in range(self.proj)] if self.nq == 2 else [1, 3, 4, 6]
        return (1 - phase, at.index(k)) if k in at else None

    def steps(self, first, last):
        for s in range(self.n + (5 if last else 0)):
            def live(k):
                return k < self.n and (k >= 0 or not first)
            yield s, live

    def part_of(self, b, m):
        part, cols = m // 2, slice((m % 2) * 512, (m % 2) * 512 + 512)
        return part, cols

    def sync(self, sp):
        w_q, w_k, w_out, nq = self.w_q, self.w_k, self.w_out, self.nq

        def load(j):
            if not isinstance(j, int) or j > 0:
                sp.wait_ge(self.w_lo, j)
            sp.dma_start(self.raw_qk[:, 0, :], w_k[:, bass.ds(j * D, D)]).then_inc(self.qk_loaded, 16)
            sp.dma_start(self.raw_qk[:, 1:1 + nq, :],
                         w_q[:, bass.ds(j * (nq * D), nq * D)].rearrange("c (h d) -> c h d", d=D))\
                .then_inc(self.qk_loaded, 16)
            if not isinstance(j, int) or j > 0:
                sp.wait_ge(self.w_o_ready, j)
            rows = w_out[bass.ds(j * (nq * D), nq * D), :].rearrange("(h d) c -> d h c", d=D)
            for half in range(2):
                sp.dma_start(self.raw_out[half * D:(half + 1) * D, :, :], rows)\
                    .then_inc(self.out_loaded, 16)

        load(0)
        with sp.Fori(1, KVH) as j:
            load(j)

    def gpsimd(self, pool):
        nc, n, nq = self.core.nc, self.n, self.nq

        def w_lo(j):
            wait(pool, self.w_hi, j + 1)
            wait(pool, self.qk_loaded, (j + 1) * 32)
            for twice in range(2):
                last = nc.gpsimd.tensor_tensor(self.w_proj[:, :, 1, twice, :], self.raw_qk[:],
                                               self.w_proj[:, :, 0, twice, :].bitcast(F32), ALU.subtract)
            last.then_inc(self.w_lo, 1)

        def v_lo(j, b, count):
            wait(pool, self.v_hi, count)
            nc.gpsimd.tensor_tensor(self.VS[b][:, :, 1, :], self.V[:, b * QT:(b + 1) * QT, bass.ds(j * D, D)],
                                    self.VS[b][:, :, 0, :].bitcast(F32), ALU.subtract).then_inc(self.v_lo, 1)

        def w_o(j, freed):
            wait(pool, self.out_loaded, (j + 1) * 32)
            wait_apart(pool, self.out_done, freed, self.pool_passed)
            nc.gpsimd.tensor_copy(self.w_o[:], self.raw_out[:]).then_inc(self.w_o_ready, 1)

        def bias(j, h, freed, count):
            if not self.alibi:
                return
            wait_apart(pool, self.maxed, freed, self.pool_passed)
            nc.gpsimd.tensor_copy(self.slope[:, h:h + 1], self.slopes[:, bass.ds(j * nq + h, 1)])\
                .then_inc(self.slope_ready, 1)
            wait_apart(pool, self.slope_ready, count, self.pool_passed)
            nc.gpsimd.tensor_scalar(self.bias[h][:], self.rel[:], self.slope[:, h:h + 1], None, ALU.mult)\
                .then_inc(self.bias_ready, 1)

        def turn(i, last):
            w_o(i, self.at(i, self.groups, 0))
            if nq == 2:
                bias(i, 1, self.at(i, n, 0), self.at(i, nq, 2))
            v_lo(i, 1, self.at(i, 2, 2))
            if not last:
                w_lo(i + 1)
                v_lo(i + 1, 0, self.at(i, 2, 3))
                bias(i + 1, 0, self.at(i, n, n - (nq - 1) * QT), self.at(i, nq, nq + 1))

        w_lo(0)
        v_lo(0, 0, 1)
        bias(0, 0, 0, 1)
        turn(0, False)
        with pool.Fori(1, KVH - 1) as i:
            turn(i, False)
        turn(KVH - 1, True)

    def scalar(self, act):
        nc, n, nq = self.core.nc, self.n, self.nq
        G, CH, PJ = self.groups, self.chunks, 2 * self.proj

        def w_hi(j, freed):
            wait(act, self.qk_loaded, (j + 1) * 32)
            wait(act, self.pj_done, freed)
            for twice in range(2):
                last = nc.scalar.activation(self.w_proj[:, :, 0, twice, :], self.raw_qk[:], ACT.Copy)
            last.then_inc(self.w_hi, 1)

        def v_hi(j, b, freed):
            wait(act, self.valued, freed)
            nc.scalar.activation(self.VS[b][:, :, 0, :], self.V[:, b * QT:(b + 1) * QT, bass.ds(j * D, D)],
                                 ACT.Copy).then_inc(self.v_hi, 1)

        def project_hi(b, m, event, freed):
            part, cols = self.part_of(b, m)
            wait(act, self.pj_done, event + 1)
            wait(act, self.scored, freed)
            out = self.KH[b] if part == 0 else self.Q[b][part - 1]
            nc.scalar.activation(out[:, cols], self.core.PJ[:], ACT.Copy).then_inc(self.pj_hi, 1)

        def turn(i, first, last):
            for s, live in self.steps(first, last):
                e = s - 2
                if live(e):
                    b, h, t = self.place(e)
                    g = t // 4
                    for c in range(self.first_chunk(e), self.end_chunk(e)):
                        wait(act, self.turned, self.at(i, CH, c + 1))
                        if t % 4 == 0:
                            wait(act, self.valued, self.at(i, G, e // 4 - 1))
                        k0 = 4 * (c - self.first_chunk(e))
                        nk = min(4, t + 1 - k0)
                        nc.scalar.activation(self.PH[g][:, k0:k0 + nk, (t % 4) * P:(t % 4 + 1) * P],
                                             self.core.TP[c % 2][:, 0:nk * P].rearrange("p (k q) -> p k q", q=P),
                                             ACT.Copy).then_inc(self.p_hi, 1)
                if s < n:
                    b, h, t = self.place(s)
                    nk = (t + 1) * P
                    wait(act, self.maxed, self.at(i, n, s + 1))
                    nc.scalar.activation(self.prob[s % 4][:, 0:nk], self.prob[s % 4][:, 0:nk], ACT.Exp,
                                         bias=self.neg_max[:, s % 4:s % 4 + 1], scale=-1.0,
                                         accum_out=self.row_sum[:, s % 16:s % 16 + 1]).then_inc(self.exped, 1)
                if pj := self.projections(s, last):
                    phase = s // (n // 2)
                    project_hi(*pj, self.at(i, PJ, self.proj * (1 + phase) + pj[1]),
                               self.at(i, n, phase * (n // 2)))
                if (s - 3) % 4 == 3 and live(s - 3):
                    q = (s - 3) // 4
                    wait(act, self.valued, self.at(i, G, q + 1))
                    wait(act, self.out_done, self.at(i, G, q - 1))
                    nc.scalar.activation(self.o_sb[q % 2][:], self.core.O[:], ACT.Copy).then_inc(self.o_copied, 1)
                if s == 5:
                    v_hi(i, 1, self.at(i, G, 0))
                if s == n // 2 - 1 and not last:
                    w_hi(i + 1, self.at(i, PJ, 2 * self.proj))
                if s == n // 2 + 5 and not last:
                    v_hi(i + 1, 0, self.at(i, G, G // 2))

        w_hi(0, 0)
        v_hi(0, 0, 0)
        for m in range(self.proj):
            project_hi(0, m, m, 0)
        turn(0, True, False)
        with act.Fori(1, KVH - 1) as i:
            turn(i, False, False)
        turn(KVH - 1, False, True)

    def vector(self, dve):
        nc, n, nq = self.core.nc, self.n, self.nq
        G, CH, PJ = self.groups, self.chunks, 2 * self.proj

        def project_lo(b, m, event):
            part, cols = self.part_of(b, m)
            wait(dve, self.pj_hi, event + 1)
            if part == 0:
                nc.vector.tensor_tensor(self.KL[b][:, cols], self.core.PJ[:],
                                        self.KH[b][:, cols].bitcast(F32), ALU.subtract).then_inc(self.pj_lo, 1)
            else:
                q = self.Q[b][part - 1][D:P, cols]
                nc.vector.tensor_tensor(q, self.core.PJ[D:P, :], q.bitcast(F32), ALU.subtract)\
                    .then_inc(self.pj_lo, 1)

        def turn(i, first, last):
            for s, live in self.steps(first, last):
                if s < n:
                    b, h, t = self.place(s)
                    nk = (t + 1) * P
                    if self.alibi and t == 0 and b == 0:
                        wait(dve, self.bias_ready, self.at(i, nq, h + 1))
                    wait(dve, self.turned, self.at(i, CH, self.end_chunk(s - 4)))
                    wait_apart(dve, self.scored, self.at(i, n, s + 1), self.passed)
                    nc.vector.tensor_tensor_reduce(
                        out=self.prob[s % 4][:, 0:nk], in0=self.core.S[s % 2][:, 0:nk],
                        in1=self.bias[h if self.alibi else 0][:, SEQ - nk:SEQ], scale=-1.0 / 8, scalar=3e38,
                        op0=ALU.add, op1=ALU.min, accum_out=self.neg_max[:, s % 4:s % 4 + 1]).then_inc(self.maxed, 1)
                e = s - 2
                if live(e):
                    b, h, t = self.place(e)
                    g = t // 4
                    for c in range(self.first_chunk(e), self.end_chunk(e)):
                        wait(dve, self.p_hi, self.at(i, CH, c + 1))
                        k0 = 4 * (c - self.first_chunk(e))
                        nk = min(4, t + 1 - k0)
                        cols = slice((t % 4) * P, (t % 4 + 1) * P)
                        nc.vector.tensor_tensor(self.PL[g][:, k0:k0 + nk, cols],
                                                self.core.TP[c % 2][:, 0:nk * P].rearrange("p (k q) -> p k q", q=P),
                                                self.PH[g][:, k0:k0 + nk, cols].bitcast(F32),
                                                ALU.subtract).then_inc(self.p_lo, 1)
                if pj := self.projections(s, last):
                    phase = s // (n // 2)
                    project_lo(*pj, self.at(i, PJ, self.proj * (1 + phase) + pj[1]))
                if (s - 4) % 4 == 3 and live(s - 4):
                    q = (s - 4) // 4
                    b, h, t = self.place(s - 4)
                    r = 4 * (q % 4)
                    wait(dve, self.exped, self.at(i, n, s - 3))
                    nc.vector.reciprocal(self.recip[:, r:r + 4], self.row_sum[:, r:r + 4]).then_inc(self.recip_done, 1)
                    wait(dve, self.recip_done, self.at(i, G, q + 1))
                    wait(dve, self.out_done, self.at(i, G, q + 1))
                    wait(dve, self.added, self.at(i, G, q))
                    for k in range(4):
                        x = self.core.x[:, b * QT + t - 3 + k, :]
                        last_add = nc.vector.scalar_tensor_tensor(
                            out=x, in0=self.core.O[:, k * C:(k + 1) * C], scalar=self.recip[:, r + k:r + k + 1],
                            in1=x, op0=ALU.mult, op1=ALU.add)
                    last_add.then_inc(self.added, 1)

        for m in range(self.proj):
            project_lo(0, m, m)
        turn(0, True, False)
        with dve.Fori(1, KVH - 1) as i:
            turn(i, False, False)
        turn(KVH - 1, False, True)

    def tensor(self, pe):
        nc, n, nq = self.core.nc, self.n, self.nq
        G, CH, PJ = self.groups, self.chunks, 2 * self.proj

        def project(b, m, event, weights):
            part, cols = self.part_of(b, m)
            tok = slice(b * SEQ + cols.start, b * SEQ + cols.stop)
            if m == 0:
                wait(pe, self.w_lo, weights)
            wait(pe, self.pj_lo, event)
            w = [self.w_proj[:, part, k, :, :].rearrange("c a d -> c (a d)") for k in range(2)]
            nc.tensor.matmul(self.core.PJ[:], w[0], self.xh[:, tok], start=True, stop=False)
            nc.tensor.matmul(self.core.PJ[:], w[1], self.xh[:, tok], start=False, stop=False)
            nc.tensor.matmul(self.core.PJ[:], w[0], self.xl[:, tok], start=False, stop=True)\
                .then_inc(self.pj_done, 1)

        def turn(i, first, last):
            for s, live in self.steps(first, last):
                if s < n:
                    b, h, t = self.place(s)
                    if s % (n // 2) == 0:
                        wait(pe, self.pj_lo, self.at(i, PJ, self.proj * (1 + b)))
                    wait(pe, self.maxed, self.at(i, n, s - 1))
                    q = self.Q[b][h][:, t * P:(t + 1) * P]
                    for k0 in range(0, (t + 1) * P, 512):
                        k1 = min(k0 + 512, (t + 1) * P)
                        out = self.core.S[s % 2][:, k0:k1]
                        nc.tensor.matmul(out, q, self.KH[b][:, k0:k1], start=True, stop=False)
                        mm = nc.tensor.matmul(out, q, self.KL[b][:, k0:k1], start=False, stop=True)
                    mm.then_inc(self.scored, 1)
                if pj := self.projections(s, last):
                    phase = s // (n // 2)
                    project(*pj, self.at(i, PJ, self.proj * (1 + phase) + pj[1]), self.at(i, 1, 1 + phase))
                e = s - 2
                if live(e):
                    b, h, t = self.place(e)
                    wait(pe, self.exped, self.at(i, n, e + 1))
                    for c in range(self.first_chunk(e), self.end_chunk(e)):
                        wait(pe, self.p_lo, self.at(i, CH, c - 1))
                        k0 = 4 * (c - self.first_chunk(e))
                        for k in range(k0, min(k0 + 4, t + 1)):
                            mm = nc.tensor.transpose(self.core.TP[c % 2][:, (k - k0) * P:(k - k0 + 1) * P],
                                                     self.prob[e % 4][:, k * P:(k + 1) * P], self.core.ident[:])
                        mm.then_inc(self.turned, 1)
                e = s - 3
                if e % 4 == 3 and live(e):
                    b, h, t = self.place(e)
                    g, q = t // 4, e // 4
                    wait(pe, self.p_lo, self.at(i, CH, self.end_chunk(e)))
                    wait(pe, self.added, self.at(i, G, q))
                    if e % (n // 2) == 3:
                        wait(pe, self.v_lo, self.at(i, 2, 1 + b))
                    for k in range(t + 1):
                        lo = max(0, k - 4 * g) * P
                        v = self.VS[b][:, k, :, :].rearrange("k a d -> k (a d)")
                        nc.tensor.matmul(self.core.O[:, lo:512], v, self.PH[g][:, k, lo:512],
                                         start=(k == 0), stop=False)
                        mm = nc.tensor.matmul(self.core.O[:, lo:512], v, self.PL[g][:, k, lo:512],
                                              start=False, stop=(k == t))
                    mm.then_inc(self.valued, 1)
                e = s - 4
                if e % 4 == 3 and live(e):
                    b, h, t = self.place(e)
                    q = e // 4
                    wait(pe, self.o_copied, self.at(i, G, q + 1))
                    if e in (3, -1 - (n - 4)):
                        wait(pe, self.w_o_ready, self.at(i, 1, 1))
                    for k in range(4):
                        mm = nc.tensor.matmul(self.core.O[:, k * C:(k + 1) * C],
                                              self.o_sb[q % 2][:, k * P:(k + 1) * P], self.w_o[:, h, :],
                                              start=True, stop=True)
                    mm.then_inc(self.out_done, 1)

        for m in range(self.proj):
            project(0, m, m, 1)
        turn(0, True, False)
        with pe.Fori(1, KVH - 1) as i:
            turn(i, False, False)
        turn(KVH - 1, False, True)


def attention_layer(core, name, nq, w_q, w_k, w_v, w_out, slopes, x_in=None, bo=None):
    nc = core.nc
    with ExitStack() as ctx:
        att = Attention(core, ctx, name, nq, w_q, w_k, w_out, slopes)

        with ExitStack() as c1:
            norm = Norm(core, c1, name + "_norm", exact=False)
            wv = c1.enter_context(nc.sbuf_tensor(f"{name}_wv", [P, KVH * D], F32))
            wvh = c1.enter_context(nc.sbuf_tensor(f"{name}_wvh", [P, KVH * D], F32R))
            wvl = c1.enter_context(nc.sbuf_tensor(f"{name}_wvl", [P, KVH * D], F32R))
            bo_row = c1.enter_context(nc.sbuf_tensor(f"{name}_bo", [1, C], F32))

            def sem(n):
                return c1.enter_context(nc.semaphore(f"{name}_{n}"))
            x_loaded, wv_loaded, bo_loaded = sem("x_loaded"), sem("wv_loaded"), sem("bo_loaded")
            wv_hi, wv_lo, const_ready, const_step = sem("wv_hi"), sem("wv_lo"), sem("const_ready"), sem("const_step")
            v_done, v_act, v_dve = sem("v_done"), sem("v_act"), sem("v_dve")
            bo_wide = sem("bo_wide")
            block = c1.enter_context(nc.Block())

            @block.sync
            def _(sp):
                if x_in is not None:
                    for g in range(4):
                        sp.dma_start(core.x[:, 4 * g:4 * g + 4, :],
                                     x_in[4 * g * P:4 * (g + 1) * P, :].rearrange("(n p) c -> p n c", p=P))\
                            .then_inc(x_loaded, 16)
                sp.dma_start(wv[:], w_v).then_inc(wv_loaded, 16)
                if bo is not None:
                    sp.dma_start(bo_row[:], bo.rearrange("(a c) -> a c", a=1)).then_inc(bo_loaded, 16)

            @block.gpsimd
            def _(pool):
                if x_in is not None:
                    nc.gpsimd.memset(core.ident[:], 0.0).then_inc(const_step, 1)
                    nc.gpsimd.memset(core.ones_row[:], 1.0).then_inc(const_step, 1)
                    pool.wait_ge(const_step, 2)
                    nc.gpsimd.affine_select(out=core.ident[:], in_=core.ident[:], compare_op=ALU.not_equal,
                                            fill=1.0, base=0, pattern=[[-1, P]], channel_multiplier=1)\
                        .then_inc(const_ready, 1)
                table = att.rel if att.alibi else att.bias[0]
                if att.alibi:
                    for h in range(att.nq * KVH):
                        nc.gpsimd.memset(att.slopes[:, h:h + 1], float(slopes[h]))
                    nc.gpsimd.iota(table[:], pattern=[[8, SEQ]], base=-8 * (SEQ - P), channel_multiplier=-8,
                                   allow_small_or_imprecise_dtypes=True).then_inc(const_step, 1)
                else:
                    nc.gpsimd.memset(table[:], 0.0).then_inc(const_step, 1)
                pool.wait_ge(const_step, 3 if x_in is not None else 1)
                nc.gpsimd.affine_select(out=table[:], in_=table[:], compare_op=ALU.is_ge, fill=MASKED,
                                        base=SEQ - P, pattern=[[-1, SEQ]], channel_multiplier=1)

            @block.vector
            def _(dve):
                if x_in is not None:
                    dve.wait_ge(x_loaded, 64)
                norm.vector(dve, att.xh, att.xl)
                dve.wait_ge(wv_hi, 1)
                nc.vector.tensor_tensor(wvl[:], wv[:], wvh[:].bitcast(F32), ALU.subtract).then_inc(wv_lo, 1)
                for t in range(NT):
                    dve.wait_ge(v_done, t + 1)
                    nc.vector.tensor_copy(att.V[:, t, 512:1024], core.S[t % 2][:, 512:1024]).then_inc(v_dve, 1)
                if bo is not None:
                    dve.wait_ge(bo_wide, 1)
                    nc.vector.tensor_tensor(core.x[:], core.x[:],
                                            core.PJ[:, 0:C].unsqueeze(1).broadcast_to([P, NT, C]), ALU.add)

            @block.scalar
            def _(act):
                norm.scalar(act, att.xh)
                act.wait_ge(wv_loaded, 16)
                nc.scalar.activation(wvh[:], wv[:], ACT.Copy).then_inc(wv_hi, 1)
                for t in range(NT):
                    act.wait_ge(v_done, t + 1)
                    nc.scalar.activation(att.V[:, t, 0:512], core.S[t % 2][:, 0:512], ACT.Copy).then_inc(v_act, 1)

            @block.tensor
            def _(pe):
                if x_in is not None:
                    pe.wait_ge(const_ready, 1)
                norm.tensor(pe)
                if bo is not None:
                    pe.wait_ge(bo_loaded, 16)
                    nc.tensor.matmul(core.PJ[:, 0:C], core.ones_row[:], bo_row[:], start=True, stop=True)\
                        .then_inc(bo_wide, 1)
                pe.wait_ge(norm.split, norm.STEPS)
                pe.wait_ge(wv_lo, 1)
                for t in range(NT):
                    if t >= 2:
                        pe.wait_ge(v_act, t - 1)
                        pe.wait_ge(v_dve, t - 1)
                    xh, xl = att.xh[:, t * P:(t + 1) * P], att.xl[:, t * P:(t + 1) * P]
                    for half in range(2):
                        cols = slice(512 * half, 512 * half + 512)
                        out = core.S[t % 2][:, cols]
                        nc.tensor.matmul(out, xh, wvh[:, cols], start=True, stop=False)
                        nc.tensor.matmul(out, xh, wvl[:, cols], start=False, stop=False)
                        mm = nc.tensor.matmul(out, xl, wvh[:, cols], start=False, stop=True)
                    mm.then_inc(v_done, 1)

        with ExitStack() as c2:
            att.loop_memory(c2)
            block = c2.enter_context(nc.Block())

            @block.sync
            def _(sp):
                att.sync(sp)

            @block.gpsimd
            def _(pool):
                att.gpsimd(pool)

            @block.scalar
            def _(act):
                att.scalar(act)

            @block.vector
            def _(dve):
                att.vector(dve)

            @block.tensor
            def _(pe):
                att.tensor(pe)


def feed_forward(core, w_gate, w_up, w_down):
    nc = core.nc
    NF = FH // P
    SCALE = float(np.float32(1.0 / 127.0))
    with ExitStack() as ctx:
        norm = Norm(core, ctx, "ffn_norm", exact=True)

        def sb(n, shape, dt=F32):
            return ctx.enter_context(nc.sbuf_tensor(f"ffn_{n}", shape, dt))

        def sem(n):
            return ctx.enter_context(nc.semaphore(f"ffn_{n}"))

        w_int = [sb(f"w_int{k}", [P, NF, P], I32) for k in range(3)]
        w_f = [sb(f"w_f{k}", [P, NF, P]) for k in range(3)]
        w_T = [sb(f"w_T{k}", [P, NF, P]) for k in range(3)]
        silu = [sb(f"silu{k}", [P, 512]) for k in range(2)]
        h = [sb(f"h{k}", [P, NF, 512]) for k in range(2)]
        loaded, dequant, turned, copied = sem("loaded"), sem("dequant"), sem("turned"), sem("copied")
        gated, upped, silued, hidden = sem("gated"), sem("upped"), sem("silued"), sem("hidden")
        downed, added = sem("downed"), sem("added")
        block = ctx.enter_context(nc.Block())

        @block.sync
        def _(sp):
            for k, w in enumerate((w_gate, w_up)):
                sp.dma_start(w_int[k][:], w.rearrange("(n f) c -> f n c", f=P)).then_inc(loaded, 16)
            sp.dma_start(w_int[2][:], w_down.rearrange("c (n f) -> c n f", f=P)).then_inc(loaded, 16)

        @block.gpsimd
        def _(pool):
            pool.wait_ge(loaded, 48)
            for k in range(3):
                nc.gpsimd.tensor_scalar(w_f[k][:], w_int[k][:], SCALE, None, ALU.mult).then_inc(dequant, 1)

        @block.tensor
        def _(pe):
            for k in range(3):
                pe.wait_ge(dequant, k + 1)
                for n in range(NF):
                    mm = nc.tensor.transpose(core.S[k % 2][:, (512 * (k // 2)) + n * P:(512 * (k // 2)) + (n + 1) * P],
                                             w_f[k][:, n, :], core.ident[:])
                mm.then_inc(turned, 1)
            norm.tensor(pe)
            pe.wait_ge(copied, 3)

            def down(c):
                pe.wait_ge(hidden, NF * (c + 1))
                if c >= 1:
                    pe.wait_ge(added, c)
                for k in range(4):
                    for f in range(NF):
                        mm = nc.tensor.matmul(core.O[:, k * C:(k + 1) * C], h[c % 2][:, f, k * P:(k + 1) * P],
                                              w_T[2][:, f, :], start=(f == 0), stop=(f == NF - 1))
                mm.then_inc(downed, 1)

            for c in range(4):
                pe.wait_ge(norm.rounded, c + 1)
                for f in range(NF):
                    u = c * NF + f
                    x = norm.xT[:, c * 512:(c + 1) * 512]
                    if u >= 2:
                        pe.wait_ge(silued, u - 1)
                        pe.wait_ge(hidden, u - 1)
                    nc.tensor.matmul(core.S[u % 2][:, 0:512], w_T[0][:, f, :], x, start=True, stop=True)\
                        .then_inc(gated, 1)
                    nc.tensor.matmul(core.S[u % 2][:, 512:1024], w_T[1][:, f, :], x, start=True, stop=True)\
                        .then_inc(upped, 1)
                if c >= 1:
                    down(c - 1)
            down(3)

        @block.scalar
        def _(act):
            for k in range(3):
                act.wait_ge(turned, k + 1)
                o = 512 * (k // 2)
                nc.scalar.activation(w_T[k][:], core.S[k % 2][:, o:o + FH].rearrange("p (n c) -> p n c", c=P),
                                     ACT.Copy).then_inc(copied, 1)
            norm.scalar(act)
            for u in range(4 * NF):
                act.wait_ge(gated, u + 1)
                if u >= 2:
                    act.wait_ge(hidden, u - 1)
                nc.scalar.activation(silu[u % 2][:], core.S[u % 2][:, 0:512], ACT.Silu).then_inc(silued, 1)

        @block.vector
        def _(dve):
            norm.vector(dve)

            def add(c):
                dve.wait_ge(downed, c + 1)
                x = core.x[:, 4 * c:4 * c + 4, :]
                nc.vector.tensor_tensor(x, core.O[:].rearrange("p (n c) -> p n c", c=C), x, ALU.add)\
                    .then_inc(added, 1)

            for c in range(4):
                for f in range(NF):
                    u = c * NF + f
                    dve.wait_ge(silued, u + 1)
                    dve.wait_ge(upped, u + 1)
                    if c >= 2:
                        dve.wait_ge(downed, c - 1)
                    nc.vector.tensor_tensor(h[c % 2][:, f, :], core.S[u % 2][:, 512:1024], silu[u % 2][:],
                                            ALU.mult).then_inc(hidden, 1)
                if c >= 1:
                    add(c - 1)
            add(3)


def mixture(core, gate_w, w1, b1, w2, b2):
    nc = core.nc
    with ExitStack() as ctx:
        norm = Norm(core, ctx, "moe_norm", exact=True)

        def sb(n, shape, dt=F32):
            return ctx.enter_context(nc.sbuf_tensor(f"moe_{n}", shape, dt))

        factor = sb("factor", [P, NT, E])
        any_kept = sb("any_kept", [1, 1], I32)

        with ExitStack() as c1:
            def sb1(n, shape, dt=F32):
                return c1.enter_context(nc.sbuf_tensor(f"gate_{n}", shape, dt))

            def sem(n):
                return c1.enter_context(nc.semaphore(f"gate_{n}"))

            gw, gwT = sb1("gw", [E, C]), sb1("gwT", [C, E])
            ones = sb1("ones", [P, P])
            order = sb1("order", [P, E])
            probs, left, score = (sb1(n, [P, NT, E]) for n in ("probs", "left", "score"))
            first, second = sb1("first", [P, NT, E]), sb1("second", [P, NT, E])
            most, total = sb1("most", [P, NT]), sb1("total", [P, NT])
            count, keep = sb1("count", [P, E]), sb1("keep", [P, E])
            loaded, consts, gw_turned, gw_copied = sem("loaded"), sem("consts"), sem("gw_turned"), sem("gw_copied")
            logits_done, shifted, exped = sem("logits_done"), sem("shifted"), sem("exped")
            counted, summed, dve_done = sem("counted"), sem("summed"), sem("dve_done")
            block = c1.enter_context(nc.Block())

            @block.sync
            def _(sp):
                sp.dma_start(gw[:], gate_w).then_inc(loaded, 16)

            @block.gpsimd
            def _(pool):
                nc.gpsimd.memset(ones[:], 1.0).then_inc(consts, 1)
                nc.gpsimd.iota(order[:], pattern=[[-1, E]], base=E, channel_multiplier=0,
                               allow_small_or_imprecise_dtypes=True).then_inc(consts, 1)

            @block.tensor
            def _(pe):
                pe.wait_ge(loaded, 16)
                nc.tensor.transpose(core.PJ[:, 0:E], gw[:], core.ident[0:E, 0:E]).then_inc(gw_turned, 1)
                norm.tensor(pe)
                pe.wait_ge(gw_copied, 1)
                pe.wait_ge(norm.rounded, norm.STEPS)
                for t in range(NT):
                    mm = nc.tensor.matmul(core.PJ[:, t * E:(t + 1) * E], norm.xT[:, t * P:(t + 1) * P], gwT[:],
                                          start=True, stop=True)
                mm.then_inc(logits_done, 1)
                pe.wait_ge(consts, 2)
                pe.wait_ge(counted, 1)
                nc.tensor.matmul(core.O[:, 0:E], ones[:], count[:], start=True, stop=True).then_inc(summed, 1)

            @block.scalar
            def _(act):
                act.wait_ge(gw_turned, 1)
                nc.scalar.activation(gwT[:], core.PJ[:, 0:E], ACT.Copy).then_inc(gw_copied, 1)
                norm.scalar(act)
                act.wait_ge(shifted, 1)
                nc.scalar.activation(probs[:], left[:], ACT.Exp).then_inc(exped, 1)

            @block.vector
            def _(dve):
                norm.vector(dve)
                n = [0]

                def then(ins):
                    n[0] += 1
                    ins.then_inc(dve_done, 1)
                    dve.wait_ge(dve_done, n[0])

                def by_row(ap):
                    return ap.unsqueeze(2).broadcast_to([P, NT, E])

                def by_expert(ap):
                    return ap.unsqueeze(1).broadcast_to([P, NT, E])

                logits = core.PJ[:, 0:NT * E].rearrange("p (n e) -> p n e", e=E)
                dve.wait_ge(logits_done, 1)
                then(nc.vector.reduce_max(most[:], logits, AX.X))
                nc.vector.tensor_tensor(left[:], logits, by_row(most[:]), ALU.subtract).then_inc(shifted, 1)
                dve.wait_ge(exped, 1)
                then(nc.vector.reduce_sum(total[:], probs[:], AX.X))
                then(nc.vector.reciprocal(total[:], total[:]))
                then(nc.vector.tensor_tensor(probs[:], probs[:], by_row(total[:]), ALU.mult))
                dve.wait_ge(consts, 2)

                def top(p, out):
                    then(nc.vector.reduce_max(most[:], p[:], AX.X))
                    then(nc.vector.tensor_tensor(score[:], p[:], by_row(most[:]), ALU.is_equal))
                    then(nc.vector.tensor_tensor(score[:], score[:], by_expert(order[:]), ALU.mult))
                    then(nc.vector.reduce_max(most[:], score[:], AX.X))
                    then(nc.vector.tensor_tensor(out[:], score[:], by_row(most[:]), ALU.is_equal))

                top(probs, first)
                then(nc.vector.scalar_tensor_tensor(out=left[:], in0=first[:], scalar=-2.0, in1=probs[:],
                                                    op0=ALU.mult, op1=ALU.add))
                top(left, second)
                then(nc.vector.tensor_tensor(first[:], first[:], second[:], ALU.add))
                nc.vector.reduce_sum(count[:], first[:].rearrange("p n e -> p e n"), AX.X).then_inc(counted, 1)
                then(nc.vector.tensor_tensor(probs[:], probs[:], first[:], ALU.mult))
                dve.wait_ge(summed, 1)
                then(nc.vector.tensor_scalar(keep[:], core.O[:, 0:E], float(CAP), None, ALU.is_le))
                then(nc.vector.tensor_tensor(factor[:], probs[:], by_expert(keep[:]), ALU.mult))
                then(nc.vector.reduce_max(any_kept[:], keep[0:1, :], AX.X))

        experts(core, norm.xT, factor, any_kept, w1, b1, w2, b2)


def experts(core, xT, factor, any_kept, w1, b1, w2, b2):
    nc = core.nc
    CH = 4
    with ExitStack() as ctx:
        def sb(n, shape, dt=F32):
            return ctx.enter_context(nc.sbuf_tensor(f"exp_{n}", shape, dt))

        def sem(n):
            return ctx.enter_context(nc.semaphore(f"exp_{n}"))

        w = [sb("w1", [P, P]), sb("w2", [P, P])]
        wT = [sb("w1T", [P, P]), sb("w2T", [P, P])]
        b1_col, b2_row = sb("b1", [P, 1]), sb("b2", [1, P])
        h = [sb("h0", [P, 512]), sb("h1", [P, 512])]
        loaded, turned, copied = sem("loaded"), sem("turned"), sem("copied")
        upped, silued, downed, added = sem("upped"), sem("silued"), sem("downed"), sem("added")
        out_bank = [core.O, core.PJ]
        block = ctx.enter_context(nc.Block())

        @block.sync
        def _(sp):
            kept = sp.value_load(any_kept[0:1, 0:1], min_val=0, max_val=1)
            with sp.If(kept > 0):
                def load(e):
                    wait(sp, downed, e * CH)
                    one = bass.ds(e, 1)
                    sp.dma_start(w[0][:], w1[one, :, :].rearrange("e f c -> (e f) c")).then_inc(loaded, 16)
                    sp.dma_start(w[1][:], w2[one, :, :].rearrange("e g f -> (e g) f")).then_inc(loaded, 16)
                    sp.dma_start(b1_col[:], b1[one, :].rearrange("e f -> f e")).then_inc(loaded, 16)
                    sp.dma_start(b2_row[:], b2[one, :]).then_inc(loaded, 16)

                load(0)
                with sp.Fori(1, E) as e:
                    load(e)

        @block.tensor
        def _(pe):
            kept = pe.value_load(any_kept[0:1, 0:1], min_val=0, max_val=1)
            with pe.If(kept > 0):
                def expert(e):
                    wait(pe, loaded, (e + 1) * 64)
                    for k in range(2):
                        mm = nc.tensor.transpose(core.TP[k][:, 0:P], w[k][:], core.ident[:])
                    mm.then_inc(turned, 1)
                    wait(pe, copied, e + 1)

                    def down(c):
                        wait(pe, silued, e * CH + (c + 1))
                        wait(pe, added, e * CH + (c - 1))
                        for k in range(4):
                            out = out_bank[c % 2][:, k * P:(k + 1) * P]
                            nc.tensor.matmul(out, h[c % 2][:, k * P:(k + 1) * P], wT[1][:], start=True, stop=False)
                            mm = nc.tensor.matmul(out, core.ones_row[:], b2_row[:], start=False, stop=True)
                        mm.then_inc(downed, 1)

                    for c in range(CH):
                        wait(pe, silued, e * CH + (c - 1))
                        nc.tensor.matmul(core.S[c % 2][:, 0:512], wT[0][:], xT[:, c * 512:(c + 1) * 512],
                                         start=True, stop=True).then_inc(upped, 1)
                        if c >= 1:
                            down(c - 1)
                    down(CH - 1)

                expert(0)
                with pe.Fori(1, E) as e:
                    expert(e)

        @block.scalar
        def _(act):
            kept = act.value_load(any_kept[0:1, 0:1], min_val=0, max_val=1)
            with act.If(kept > 0):
                def expert(e):
                    wait(act, turned, e + 1)
                    wait(act, downed, e * CH)
                    for k in range(2):
                        last = nc.scalar.activation(wT[k][:], core.TP[k][:, 0:P], ACT.Copy)
                    last.then_inc(copied, 1)
                    for c in range(CH):
                        wait(act, upped, e * CH + (c + 1))
                        wait(act, downed, e * CH + (c - 1))
                        nc.scalar.activation(h[c % 2][:], core.S[c % 2][:, 0:512], ACT.Silu, bias=b1_col[:, 0:1])\
                            .then_inc(silued, 1)

                expert(0)
                with act.Fori(1, E) as e:
                    expert(e)

        @block.vector
        def _(dve):
            kept = dve.value_load(any_kept[0:1, 0:1], min_val=0, max_val=1)
            with dve.If(kept > 0):
                def expert(e):
                    for c in range(CH):
                        wait(dve, downed, e * CH + (c + 1))
                        wait(dve, added, e * CH + c)
                        for k in range(4):
                            t = 4 * c + k
                            last = nc.vector.scalar_tensor_tensor(
                                out=core.x[:, t, :], in0=out_bank[c % 2][:, k * P:(k + 1) * P],
                                scalar=factor[:, t, bass.ds(e, 1)], in1=core.x[:, t, :], op0=ALU.mult, op1=ALU.add)
                        last.then_inc(added, 1)

                expert(0)
                with dve.Fori(1, E) as e:
                    expert(e)


def store(core, out):
    nc = core.nc
    with nc.semaphore("stored") as stored, nc.Block() as block:
        @block.sync
        def _(sp):
            sp.dma_start(out.rearrange("(n p) c -> p n c", p=P), core.x[:]).then_inc(stored, 16)
            sp.wait_ge(stored, 16)


def program(nc, inputs, out):
    with ExitStack() as ctx:
        core = Core(nc, ctx)
        a = inputs
        w0 = a["L0_attn_W_qkv"]
        nq0 = 2 * KVH * D
        attention_layer(core, "a0", 2, w0[:, 0:nq0], w0[:, nq0:nq0 + KVH * D], w0[:, nq0 + KVH * D:],
                        a["L0_attn_W_out"], alibi_slopes(2 * KVH),
                        x_in=a["L0_attn_inputs"].rearrange("b s c -> (b s) c"))
        feed_forward(core, a["L0_ffn_w_gate"], a["L0_ffn_w_up"], a["L0_ffn_w_down"])
        attention_layer(core, "a1", 1, a["L1_attn_Wq"], a["L1_attn_Wk"], a["L1_attn_Wv"], a["L1_attn_Wo"],
                        None, bo=a["L1_attn_bo"])
        mixture(core, a["L1_ffn_gate_w"], a["L1_ffn_w1"], a["L1_ffn_b1"], a["L1_ffn_w2"], a["L1_ffn_b2"])
        store(core, out.rearrange("b s c -> (b s) c"))


_INS = ['L0_attn_inputs', 'L0_attn_W_qkv', 'L0_attn_W_out', 'L0_ffn_w_gate', 'L0_ffn_w_up', 'L0_ffn_w_down',
        'L1_attn_Wq', 'L1_attn_Wk', 'L1_attn_Wv', 'L1_attn_Wo', 'L1_attn_bo',
        'L1_ffn_gate_w', 'L1_ffn_w1', 'L1_ffn_b1', 'L1_ffn_w2', 'L1_ffn_b2']


def kernel(**inputs):
    import concourse.bacc as bacc
    from concourse.bass_utils import run_bass_kernel_spmd

    nc = bacc.Bacc("TRN2", target_bir_lowering=False, num_devices=1,
                   dynamic_dma_scratch_size=1024)
    arrays, aps = {}, {}
    for name in _INS:
        a = np.ascontiguousarray(inputs[name])
        arrays[name] = a
        aps[name] = nc.dram_tensor(name, a.shape, mybir.dt.from_np(a.dtype), kind="ExternalInput").ap()
    out = nc.dram_tensor("out", (BATCH, SEQ, C), F32, kind="ExternalOutput").ap()
    program(nc, aps, out)
    r = run_bass_kernel_spmd(nc, [arrays], core_ids=[0])
    return r.results[0]["out"]
```

```python
import numpy as np
import concourse.bass as bass
from concourse import mybir
from contextlib import ExitStack

F32 = mybir.dt.float32
F32R = mybir.dt.float32r
I32 = mybir.dt.int32
ALU = mybir.AluOpType
ACT = mybir.ActivationFunctionType
AX = mybir.AxisListType

P = 128
C = 128
BATCH = 2
SEQ = 1024
TOK = BATCH * SEQ
NT = TOK // P
QT = SEQ // P
D = 64
KVH = 16
FH = 384
E = 8
SCORE_BANKS = [[0], [1], [0], [2], [0, 1], [1, 2], [0, 1], [1, 2]]
LAG = 3
CAP = int(1.25 * TOK / E)
EPS = 1e-5
MASKED = -1e34
LANES = 4


def alibi_slopes(n):
    base = 2.0 ** (-2.0 ** (-(np.log2(n) - 3)))
    return (base ** np.arange(1, n + 1, dtype=np.float32)).astype(np.float32)


class Core:

    def __init__(self, nc, ctx):
        self.nc = nc

        def sb(name, shape, dt=F32):
            return ctx.enter_context(nc.sbuf_tensor(name, shape, dt))

        def ps(name, cols):
            return ctx.enter_context(nc.psum_tensor(name, [P, cols], F32))

        self.x = sb("x", [P, NT, C])
        self.ident = sb("ident", [P, P])
        self.ones_row = sb("ones_row", [1, P])
        self.scores = ps("scores", 2048)
        self.S = [self.scores[:, 0:1024], self.scores[:, 1024:2048]]
        self.TP = [ps("TP0", 512), ps("TP1", 512), self.scores[:, 1536:2048]]
        self.O = ps("O", 512)
        self.PJ = ps("PJ", 512)


def wait_apart(eng, sem, value, passed):
    wait(eng, sem, value)
    if not isinstance(value, int):
        eng.sem_inc(passed, 1)


def wait(eng, sem, value):
    if isinstance(value, int) and value <= 0:
        return
    eng.wait_ge(sem, value)


class Norm:

    def __init__(self, core, ctx, name, exact):
        nc = core.nc
        self.core, self.exact = core, exact

        def sb(n, shape, dt=F32):
            return ctx.enter_context(nc.sbuf_tensor(f"{name}_{n}", shape, dt))

        def sem(n):
            return ctx.enter_context(nc.semaphore(f"{name}_{n}"))

        self.xn = sb("xn", [P, NT, C])
        self.sq = sb("sq", [P, LANES, C])
        self.mean = sb("mean", [P, NT])
        self.var = sb("var", [P, NT])
        self.std = sb("std", [P, NT])
        self.rstd = sb("rstd", [P, NT])
        self.tmp = sb("tmp", [P, NT])
        if exact:
            self.xT = sb("xT", [P, TOK])
        self.dve_done = sem("dve_done")
        self.var_ready = sem("var_ready")
        self.std_ready = sem("std_ready")
        self.xn_ready = sem("xn_ready")
        self.turned = sem("turned")
        self.rounded = sem("rounded")
        self.split = sem("split")

    STEPS = NT // LANES

    def vector(self, dve, hi=None, lo=None):
        nc, x = self.core.nc, self.core.x
        n = [0]

        def then(ins):
            n[0] += 1
            ins.then_inc(self.dve_done, 1)
            dve.wait_ge(self.dve_done, n[0])

        def wide(ap):
            return ap.unsqueeze(2).broadcast_to([P, LANES, C])

        for g in range(self.STEPS):
            s = slice(g * LANES, (g + 1) * LANES)
            then(nc.vector.reduce_sum(self.mean[:, s], x[:, s, :], axis=AX.X))
            then(nc.vector.tensor_scalar(self.mean[:, s], self.mean[:, s], 1.0 / C, None, ALU.mult))
            then(nc.vector.tensor_tensor(self.xn[:, s, :], x[:, s, :], wide(self.mean[:, s]), ALU.subtract))
            then(nc.vector.tensor_tensor(self.sq[:], self.xn[:, s, :], self.xn[:, s, :], ALU.mult))
            then(nc.vector.reduce_sum(self.var[:, s], self.sq[:], axis=AX.X))
            nc.vector.tensor_scalar(self.var[:, s], self.var[:, s], 1.0 / C, EPS, ALU.mult, ALU.add)\
                .then_inc(self.var_ready, 1)
        for g in range(self.STEPS):
            s = slice(g * LANES, (g + 1) * LANES)
            dve.wait_ge(self.std_ready, g + 1)
            then(nc.vector.reciprocal(self.rstd[:, s], self.std[:, s]))
            then(nc.vector.tensor_tensor(self.tmp[:, s], self.rstd[:, s], self.rstd[:, s], ALU.mult))
            then(nc.vector.tensor_tensor(self.tmp[:, s], self.tmp[:, s], self.var[:, s], ALU.mult))
            then(nc.vector.tensor_scalar(self.tmp[:, s], self.tmp[:, s], -0.5, 1.5, ALU.mult, ALU.add))
            then(nc.vector.tensor_tensor(self.rstd[:, s], self.rstd[:, s], self.tmp[:, s], ALU.mult))
            nc.vector.tensor_tensor(self.xn[:, s, :], self.xn[:, s, :], wide(self.rstd[:, s]), ALU.mult)\
                .then_inc(self.xn_ready, 1)
        if not self.exact:
            for g in range(self.STEPS):
                cols = slice(g * 512, (g + 1) * 512)
                dve.wait_ge(self.rounded, g + 1)
                nc.vector.tensor_tensor(lo[:, cols], self.core.TP[g % 2][:], hi[:, cols].bitcast(F32),
                                        ALU.subtract).then_inc(self.split, 1)

    def scalar(self, act, hi=None):
        nc = self.core.nc
        for g in range(self.STEPS):
            s = slice(g * LANES, (g + 1) * LANES)
            act.wait_ge(self.var_ready, g + 1)
            nc.scalar.activation(self.std[:, s], self.var[:, s], ACT.Sqrt).then_inc(self.std_ready, 1)
        for g in range(self.STEPS):
            act.wait_ge(self.turned, g + 1)
            out = self.xT if self.exact else hi
            nc.scalar.activation(out[:, g * 512:(g + 1) * 512], self.core.TP[g % 2][:], ACT.Copy)\
                .then_inc(self.rounded, 1)

    def tensor(self, pe):
        nc = self.core.nc
        for g in range(self.STEPS):
            pe.wait_ge(self.xn_ready, g + 1)
            if g >= 2:
                pe.wait_ge(self.rounded if self.exact else self.split, g - 1)
            for n in range(LANES):
                last = nc.tensor.transpose(self.core.TP[g % 2][:, n * P:(n + 1) * P],
                                           self.xn[:, g * LANES + n, :], self.core.ident[:])
            last.then_inc(self.turned, 1)


class Attention:

    def __init__(self, core, ctx, name, nq, w_q, w_k, w_out, slopes):
        nc = core.nc
        self.core, self.nq, self.name = core, nq, name
        self.w_q, self.w_k, self.w_out = w_q, w_k, w_out
        self.alibi = slopes is not None
        self.n = 2 * nq * QT
        self.groups = self.n // 4
        self.chunks = 12 * self.n // QT
        self.parts = 1 + nq
        self.proj = 2 * self.parts
        self.when = {2: [2, 4, 6, 10, 12, 15], 1: [1, 3, 5, 6]}[nq]
        self.weights_step = self.when[-1]

        def sb(n, shape, dt=F32):
            return ctx.enter_context(nc.sbuf_tensor(f"{name}_{n}", shape, dt))

        def sem(n):
            return ctx.enter_context(nc.semaphore(f"{name}_{n}"))

        self.xh = sb("xh", [P, TOK], F32R)
        self.xl = sb("xl", [P, TOK], F32R)
        self.V = sb("V", [P, NT, KVH * D])
        if self.alibi:
            self.rel = sb("rel", [P, SEQ])
            self.slopes = sb("slopes", [P, nq * KVH])
            self.slope = sb("slope", [P, nq])
        self.bias = [sb(f"bias{h}", [P, SEQ]) for h in range(nq if self.alibi else 1)]

    def loop_memory(self, ctx):
        nc, name, nq = self.core.nc, self.name, self.nq

        def sb(n, shape, dt=F32):
            return ctx.enter_context(nc.sbuf_tensor(f"{name}_{n}", shape, dt))

        def sem(n):
            return ctx.enter_context(nc.semaphore(f"{name}_{n}"))

        self.raw_qk = sb("raw_qk", [P, self.parts, D])
        self.raw_out = sb("raw_out", [P, nq, C])
        self.w_proj = sb("w_proj", [P, self.parts, 2, 2, D], F32R)
        self.w_o = sb("w_o", [P, nq, C])
        self.KH = [sb(f"KH{b}", [P, SEQ], F32R) for b in range(2)]
        self.KL = [sb(f"KL{b}", [P, SEQ], F32R) for b in range(2)]
        self.Q = [[sb(f"Q{b}{h}", [P, SEQ], F32R) for h in range(nq)] for b in range(2)]
        self.VS = [sb(f"VS{b}", [P, QT, 2, D], F32R) for b in range(2)]
        self.prob = [sb(f"prob{i}", [P, SEQ]) for i in range(4)]
        self.neg_max = sb("neg_max", [P, 4])
        self.row_sum = sb("row_sum", [P, 16])
        self.recip = sb("recip", [P, 16])
        self.PH = [sb(f"PH{g}", [P, 4 * (g + 1), 512], F32R) for g in range(2)]
        self.PL = [sb(f"PL{g}", [P, 4 * (g + 1), 512], F32R) for g in range(2)]
        self.pj_copy = [sb(f"pj_copy{k}", [P, 512]) for k in range(2)]
        self.o_sb = [sb(f"o_sb{i}", [P, 512]) for i in range(2)]

        self.qk_loaded = sem("qk_loaded")
        self.out_loaded = sem("out_loaded")
        self.w_hi = sem("w_hi")
        self.w_lo = sem("w_lo")
        self.w_o_ready = sem("w_o_ready")
        self.v_hi = sem("v_hi")
        self.v_lo = sem("v_lo")
        self.bias_ready = sem("bias_ready")
        self.slope_ready = sem("slope_ready")
        self.passed = sem("passed")
        self.pool_passed = sem("pool_passed")
        self.pj_done = sem("pj_done")
        self.pj_hi = sem("pj_hi")
        self.pj_lo = sem("pj_lo")
        self.scored = sem("scored")
        self.maxed = sem("maxed")
        self.exped = sem("exped")
        self.turned = sem("turned")
        self.p_hi = sem("p_hi")
        self.p_lo = sem("p_lo")
        self.valued = sem("valued")
        self.o_copied = sem("o_copied")
        self.out_done = sem("out_done")
        self.recip_done = sem("recip_done")
        self.added = sem("added")

    def place(self, s):
        s %= self.n
        return s // (self.nq * QT), (s // QT) % self.nq, s % QT

    def first_chunk(self, s):
        t = s % QT
        return (s // QT) * 12 + (t if t < 4 else 4 + 2 * (t - 4))

    def score_banks(self, s):
        return SCORE_BANKS[s % QT]

    def score_columns(self, s):
        first = min(self.score_banks(s)) * 512
        return self.core.scores[:, first:first + (s % QT + 1) * P]

    def bank_freed(self, s, bank):
        return max(k for k in range(s - 4, s) if bank in self.score_banks(k)) + 1

    def end_chunk(self, s):
        return self.first_chunk(s) + (1 if s % QT < 4 else 2)

    def at(self, i, per_turn, count):
        return i * per_turn + count

    def projections(self, s, last):
        half = self.n // 2
        phase, k = s // half, s % half
        if s >= self.n or (phase == 1 and last) or k not in self.when:
            return None
        return 1 - phase, self.when.index(k)

    def steps(self, first, last):
        for s in range(self.n + (LAG + 4 if last else 0)):
            def live(k):
                return k < self.n and (k >= 0 or not first)
            yield s, live

    def part_of(self, b, m):
        part, cols = m // 2, slice((m % 2) * 512, (m % 2) * 512 + 512)
        return part, cols

    def sync(self, sp):
        w_q, w_k, w_out, nq = self.w_q, self.w_k, self.w_out, self.nq

        def load(j):
            if not isinstance(j, int) or j > 0:
                sp.wait_ge(self.w_lo, j)
            sp.dma_start(self.raw_qk[:, 0, :], w_k[:, bass.ds(j * D, D)]).then_inc(self.qk_loaded, 16)
            sp.dma_start(self.raw_qk[:, 1:1 + nq, :],
                         w_q[:, bass.ds(j * (nq * D), nq * D)].rearrange("c (h d) -> c h d", d=D))\
                .then_inc(self.qk_loaded, 16)
            if not isinstance(j, int) or j > 0:
                sp.wait_ge(self.w_o_ready, j)
            rows = w_out[bass.ds(j * (nq * D), nq * D), :].rearrange("(h d) c -> d h c", d=D)
            for half in range(2):
                sp.dma_start(self.raw_out[half * D:(half + 1) * D, :, :], rows)\
                    .then_inc(self.out_loaded, 16)

        load(0)
        with sp.Fori(1, KVH) as j:
            load(j)

    def gpsimd(self, pool):
        nc, n, nq = self.core.nc, self.n, self.nq
        PJ = 2 * self.proj

        def w_lo(j, before):
            wait(pool, *before)
            wait(pool, self.w_hi, j + 1)
            wait(pool, self.qk_loaded, (j + 1) * 32)
            for twice in range(2):
                last = nc.gpsimd.tensor_tensor(self.w_proj[:, :, 1, twice, :], self.raw_qk[:],
                                               self.w_proj[:, :, 0, twice, :].bitcast(F32), ALU.subtract)
            last.then_inc(self.w_lo, 1)
            return self.w_lo, j + 1

        def v_lo(j, b, count, before):
            wait(pool, *before)
            wait(pool, self.v_hi, count)
            nc.gpsimd.tensor_tensor(self.VS[b][:, :, 1, :], self.V[:, b * QT:(b + 1) * QT, bass.ds(j * D, D)],
                                    self.VS[b][:, :, 0, :].bitcast(F32), ALU.subtract).then_inc(self.v_lo, 1)
            return self.v_lo, count

        def w_o(j, freed, before):
            wait(pool, *before)
            wait(pool, self.out_loaded, (j + 1) * 32)
            wait_apart(pool, self.out_done, freed, self.pool_passed)
            nc.gpsimd.tensor_copy(self.w_o[:], self.raw_out[:]).then_inc(self.w_o_ready, 1)
            return self.w_o_ready, j + 1

        def bias(j, h, freed, count, before):
            wait(pool, *before)
            wait_apart(pool, self.maxed, freed, self.pool_passed)
            nc.gpsimd.tensor_copy(self.slope[:, h:h + 1], self.slopes[:, bass.ds(j * nq + h, 1)])\
                .then_inc(self.slope_ready, 1)
            wait_apart(pool, self.slope_ready, count, self.pool_passed)
            nc.gpsimd.tensor_tensor(self.bias[h][:], self.rel[:],
                                    self.slope[:, h:h + 1].broadcast_to([P, SEQ]), ALU.mult)\
                .then_inc(self.bias_ready, 1)
            return self.bias_ready, count

        def project_lo(b, m, event, before):
            part, cols = self.part_of(b, m)
            wait(pool, *before)
            wait(pool, self.pj_hi, event + 1)
            if part == 0:
                hi, lo, rows = self.KH[b][:, cols], self.KL[b][:, cols], slice(0, P)
            else:
                hi = lo = self.Q[b][part - 1][D:P, cols]
                rows = slice(D, P)
            nc.gpsimd.tensor_tensor(lo, self.pj_copy[m % 2][rows, :], hi.bitcast(F32), ALU.subtract)\
                .then_inc(self.pj_lo, 1)
            return self.pj_lo, event + 1

        def turn(i, last, before):
            for s in range(n):
                if pj := self.projections(s, last):
                    phase = s // (n // 2)
                    before = project_lo(*pj, self.at(i, PJ, self.proj * (1 + phase) + pj[1]), before)
                if s == 1 and nq == 2:
                    before = bias(i, 1, self.at(i, n, 0), self.at(i, nq, 2), before)
                if s == 7:
                    before = w_o(i, self.at(i, self.groups, 0), before)
                if s == 6:
                    before = v_lo(i, 1, self.at(i, 2, 2), before)
                if last:
                    continue
                if s == self.weights_step:
                    before = w_lo(i + 1, before)
                if s == n // 2 + 6:
                    before = v_lo(i + 1, 0, self.at(i, 2, 3), before)
                if self.alibi and s == n - (nq - 1) * QT + 2:
                    before = bias(i + 1, 0, self.at(i, n, n - (nq - 1) * QT), self.at(i, nq, nq + 1), before)

        before = w_lo(0, (self.w_lo, 0))
        before = v_lo(0, 0, 1, before)
        if self.alibi:
            before = bias(0, 0, 0, 1, before)
        for m in range(self.proj):
            before = project_lo(0, m, m, before)
        turn(0, False, before)

        def end_of_turn(i):
            late_projection = self.when[-1] > 6
            return (self.pj_lo, self.at(i, PJ, self.proj)) if late_projection else (self.v_lo, self.at(i, 2, 1))

        with pool.Fori(1, KVH - 1) as i:
            turn(i, False, end_of_turn(i))
        turn(KVH - 1, True, end_of_turn(KVH - 1))

    def scalar(self, act):
        nc, n, nq = self.core.nc, self.n, self.nq
        G, CH, PJ = self.groups, self.chunks, 2 * self.proj

        def w_hi(j, freed):
            wait(act, self.qk_loaded, (j + 1) * 32)
            wait(act, self.pj_done, freed)
            for twice in range(2):
                last = nc.scalar.activation(self.w_proj[:, :, 0, twice, :], self.raw_qk[:], ACT.Copy)
            last.then_inc(self.w_hi, 1)

        def v_hi(j, b, freed):
            wait(act, self.valued, freed)
            nc.scalar.activation(self.VS[b][:, :, 0, :], self.V[:, b * QT:(b + 1) * QT, bass.ds(j * D, D)],
                                 ACT.Copy).then_inc(self.v_hi, 1)

        def project_hi(b, m, event, freed):
            part, cols = self.part_of(b, m)
            wait(act, self.pj_done, event + 1)
            wait(act, self.scored, freed)
            out = self.KH[b] if part == 0 else self.Q[b][part - 1]
            nc.scalar.activation(out[:, cols], self.core.PJ[:], ACT.Copy)
            wait(act, self.pj_lo, event - 1)
            rows = slice(0, P) if part == 0 else slice(D, P)
            nc.scalar.activation(self.pj_copy[m % 2][rows, :], self.core.PJ[rows, :], ACT.Copy).then_inc(self.pj_hi, 1)

        def round_probs(i, e, c):
            b, h, t = self.place(e)
            g = t // 4
            wait(act, self.turned, self.at(i, CH, c + 1))
            if t % 4 == 0:
                wait(act, self.valued, self.at(i, G, e // 4 - 1))
            k0 = 4 * (c - self.first_chunk(e))
            nk = min(4, t + 1 - k0)
            nc.scalar.activation(self.PH[g][:, k0:k0 + nk, (t % 4) * P:(t % 4 + 1) * P],
                                 self.core.TP[c % 3][:, 0:nk * P].rearrange("p (k q) -> p k q", q=P),
                                 ACT.Copy).then_inc(self.p_hi, 1)

        def turn(i, first, last):
            for s, live in self.steps(first, last):
                if live(s - LAG):
                    round_probs(i, s - LAG, self.first_chunk(s - LAG))
                e = s - 1
                if live(e):
                    b, h, t = self.place(e)
                    nk = (t + 1) * P
                    wait(act, self.maxed, self.at(i, n, e + 1))
                    nc.scalar.activation(self.prob[e % 4][:, 0:nk], self.prob[e % 4][:, 0:nk], ACT.Exp,
                                         bias=self.neg_max[:, e % 4:e % 4 + 1], scale=-1.0,
                                         accum_out=self.row_sum[:, e % 16:e % 16 + 1]).then_inc(self.exped, 1)
                e = s - LAG - 3
                if e % 4 == 3 and live(e):
                    q = e // 4
                    wait(act, self.valued, self.at(i, G, q + 1))
                    wait(act, self.out_done, self.at(i, G, q - 1))
                    nc.scalar.activation(self.o_sb[q % 2][:], self.core.O[:], ACT.Copy).then_inc(self.o_copied, 1)
                if pj := self.projections(s, last):
                    phase = s // (n // 2)
                    project_hi(*pj, self.at(i, PJ, self.proj * (1 + phase) + pj[1]),
                               self.at(i, n, phase * (n // 2)))
                if live(s - LAG):
                    for c in range(self.first_chunk(s - LAG) + 1, self.end_chunk(s - LAG)):
                        round_probs(i, s - LAG, c)
                if s == 6:
                    v_hi(i, 1, self.at(i, G, 0))
                if s == self.weights_step and not last:
                    w_hi(i + 1, self.at(i, PJ, 2 * self.proj))
                if s == n // 2 + 6 and not last:
                    v_hi(i + 1, 0, self.at(i, G, G // 2))

        w_hi(0, 0)
        v_hi(0, 0, 0)
        for m in range(self.proj):
            project_hi(0, m, m, 0)
        turn(0, True, False)
        with act.Fori(1, KVH - 1) as i:
            turn(i, False, False)
        turn(KVH - 1, False, True)

    def vector(self, dve):
        nc, n, nq = self.core.nc, self.n, self.nq
        G, CH, PJ = self.groups, self.chunks, 2 * self.proj

        def rest_of_probs(i, e, c):
            b, h, t = self.place(e)
            g = t // 4
            wait(dve, self.p_hi, self.at(i, CH, c + 1))
            k0 = 4 * (c - self.first_chunk(e))
            nk = min(4, t + 1 - k0)
            cols = slice((t % 4) * P, (t % 4 + 1) * P)
            nc.vector.tensor_tensor(self.PL[g][:, k0:k0 + nk, cols],
                                    self.core.TP[c % 3][:, 0:nk * P].rearrange("p (k q) -> p k q", q=P),
                                    self.PH[g][:, k0:k0 + nk, cols].bitcast(F32), ALU.subtract).then_inc(self.p_lo, 1)

        def turn(i, first, last):
            for s, live in self.steps(first, last):
                if s < n:
                    b, h, t = self.place(s)
                    nk = (t + 1) * P
                    if self.alibi and t == 0 and b == 0:
                        wait(dve, self.bias_ready, self.at(i, nq, h + 1))
                    wait(dve, self.turned, self.at(i, CH, self.end_chunk(s - 4)))
                    wait_apart(dve, self.scored, self.at(i, n, s + 1), self.passed)
                    nc.vector.tensor_tensor_reduce(
                        out=self.prob[s % 4][:, 0:nk], in0=self.score_columns(s),
                        in1=self.bias[h if self.alibi else 0][:, SEQ - nk:SEQ], scale=-1.0 / 8, scalar=3e38,
                        op0=ALU.add, op1=ALU.min, accum_out=self.neg_max[:, s % 4:s % 4 + 1]).then_inc(self.maxed, 1)
                if live(s - LAG):
                    rest_of_probs(i, s - LAG, self.first_chunk(s - LAG))
                e = s - LAG - 4
                if e % 4 == 3 and live(e):
                    q = e // 4
                    b, h, t = self.place(e)
                    r = 4 * (q % 4)
                    wait(dve, self.exped, self.at(i, n, e + 1))
                    nc.vector.reciprocal(self.recip[:, r:r + 4], self.row_sum[:, r:r + 4]).then_inc(self.recip_done, 1)
                    wait(dve, self.recip_done, self.at(i, G, q + 1))
                    wait(dve, self.out_done, self.at(i, G, q + 1))
                    wait(dve, self.added, self.at(i, G, q))
                    for k in range(4):
                        x = self.core.x[:, b * QT + t - 3 + k, :]
                        last_add = nc.vector.scalar_tensor_tensor(
                            out=x, in0=self.core.O[:, k * C:(k + 1) * C], scalar=self.recip[:, r + k:r + k + 1],
                            in1=x, op0=ALU.mult, op1=ALU.add)
                    last_add.then_inc(self.added, 1)
                if live(s - LAG):
                    for c in range(self.first_chunk(s - LAG) + 1, self.end_chunk(s - LAG)):
                        rest_of_probs(i, s - LAG, c)

        turn(0, True, False)
        with dve.Fori(1, KVH - 1) as i:
            turn(i, False, False)
        turn(KVH - 1, False, True)

    def tensor(self, pe):
        nc, n, nq = self.core.nc, self.n, self.nq
        G, CH, PJ = self.groups, self.chunks, 2 * self.proj

        def project(b, m, event, weights):
            part, cols = self.part_of(b, m)
            tok = slice(b * SEQ + cols.start, b * SEQ + cols.stop)
            if m == 0:
                wait(pe, self.w_lo, weights)
            wait(pe, self.pj_hi, event)
            w = [self.w_proj[:, part, k, :, :].rearrange("c a d -> c (a d)") for k in range(2)]
            nc.tensor.matmul(self.core.PJ[:], w[0], self.xh[:, tok], start=True, stop=False)
            nc.tensor.matmul(self.core.PJ[:], w[1], self.xh[:, tok], start=False, stop=False)
            nc.tensor.matmul(self.core.PJ[:], w[0], self.xl[:, tok], start=False, stop=True)\
                .then_inc(self.pj_done, 1)

        def turn_probs(i, e, c):
            b, h, t = self.place(e)
            wait(pe, self.exped, self.at(i, n, e + 1))
            wait(pe, self.p_lo, self.at(i, CH, c - 2))
            k0 = 4 * (c - self.first_chunk(e))
            for k in range(k0, min(k0 + 4, t + 1)):
                mm = nc.tensor.transpose(self.core.TP[c % 3][:, (k - k0) * P:(k - k0 + 1) * P],
                                         self.prob[e % 4][:, k * P:(k + 1) * P], self.core.ident[:])
            mm.then_inc(self.turned, 1)

        def scores(i, s):
            b, h, t = self.place(s)
            if t == 0:
                wait(pe, self.pj_lo, self.at(i, PJ, self.proj * (1 + b) - 2 * (nq - 1 - h)))
            q = self.Q[b][h][:, t * P:(t + 1) * P]
            for j in sorted(range(len(self.score_banks(s))),
                            key=lambda j: self.bank_freed(s, self.score_banks(s)[j])):
                wait(pe, self.maxed, self.at(i, n, self.bank_freed(s, self.score_banks(s)[j])))
                k0, k1 = j * 512, min((j + 1) * 512, (t + 1) * P)
                out = self.score_columns(s)[:, k0:k1]
                nc.tensor.matmul(out, q, self.KH[b][:, k0:k1], start=True, stop=False)
                mm = nc.tensor.matmul(out, q, self.KL[b][:, k0:k1], start=False, stop=True)
            mm.then_inc(self.scored, 1)

        def values(i, e, first_tile, end_tile):
            b, h, t = self.place(e)
            g, q = t // 4, e // 4
            if first_tile == 0:
                wait(pe, self.p_lo, self.at(i, CH, self.end_chunk(e)))
                wait(pe, self.added, self.at(i, G, q))
                if e % (n // 2) == 3:
                    wait(pe, self.v_lo, self.at(i, 2, 2 * (e // n) + 1 + b))
            for k in range(first_tile, end_tile):
                lo = max(0, k - 4 * g) * P
                v = self.VS[b][:, k, :, :].rearrange("k a d -> k (a d)")
                nc.tensor.matmul(self.core.O[:, lo:512], v, self.PH[g][:, k, lo:512],
                                 start=(k == 0), stop=False)
                mm = nc.tensor.matmul(self.core.O[:, lo:512], v, self.PL[g][:, k, lo:512],
                                      start=False, stop=(k == t))
            if end_tile == t + 1:
                mm.then_inc(self.valued, 1)

        def project_out(i, e):
            b, h, t = self.place(e)
            q = e // 4
            wait(pe, self.o_copied, self.at(i, G, q + 1))
            if e == 3:
                wait(pe, self.w_o_ready, self.at(i, 1, 1))
            for k in range(4):
                mm = nc.tensor.matmul(self.core.O[:, k * C:(k + 1) * C],
                                      self.o_sb[q % 2][:, k * P:(k + 1) * P], self.w_o[:, h, :],
                                      start=True, stop=True)
            mm.then_inc(self.out_done, 1)

        def turn(i, first, last):
            for s, live in self.steps(first, last):
                if live(s - LAG):
                    turn_probs(i, s - LAG, self.first_chunk(s - LAG))
                if s < n:
                    scores(i, s)
                e = s - LAG - 4
                if e % 4 == 3 and live(e):
                    project_out(i, e)
                e = s - LAG - 3
                if e % QT == QT - 1 and live(e):
                    values(i, e, QT // 2, QT)
                if pj := self.projections(s, last):
                    phase = s // (n // 2)
                    project(*pj, self.at(i, PJ, self.proj * (1 + phase) + pj[1]), self.at(i, 1, 1 + phase))
                e = s - LAG - 2
                if e % 4 == 3 and live(e):
                    values(i, e, 0, QT // 2)
                if live(s - LAG):
                    for c in range(self.first_chunk(s - LAG) + 1, self.end_chunk(s - LAG)):
                        turn_probs(i, s - LAG, c)

        for m in range(self.proj):
            project(0, m, m, 1)
        turn(0, True, False)
        with pe.Fori(1, KVH - 1) as i:
            turn(i, False, False)
        turn(KVH - 1, False, True)


def attention_layer(core, name, nq, w_q, w_k, w_v, w_out, slopes, x_in=None, bo=None):
    nc = core.nc
    with ExitStack() as ctx:
        att = Attention(core, ctx, name, nq, w_q, w_k, w_out, slopes)

        with ExitStack() as c1:
            norm = Norm(core, c1, name + "_norm", exact=False)
            wv = c1.enter_context(nc.sbuf_tensor(f"{name}_wv", [P, KVH * D], F32))
            wvh = c1.enter_context(nc.sbuf_tensor(f"{name}_wvh", [P, KVH * D], F32R))
            wvl = c1.enter_context(nc.sbuf_tensor(f"{name}_wvl", [P, KVH * D], F32R))
            bo_row = c1.enter_context(nc.sbuf_tensor(f"{name}_bo", [1, C], F32))

            def sem(n):
                return c1.enter_context(nc.semaphore(f"{name}_{n}"))
            x_loaded, wv_loaded, bo_loaded = sem("x_loaded"), sem("wv_loaded"), sem("bo_loaded")
            wv_hi, wv_lo, const_ready, const_step = sem("wv_hi"), sem("wv_lo"), sem("const_ready"), sem("const_step")
            v_done, v_act, v_dve = sem("v_done"), sem("v_act"), sem("v_dve")
            bo_wide = sem("bo_wide")
            block = c1.enter_context(nc.Block())

            @block.sync
            def _(sp):
                if x_in is not None:
                    for g in range(4):
                        sp.dma_start(core.x[:, 4 * g:4 * g + 4, :],
                                     x_in[4 * g * P:4 * (g + 1) * P, :].rearrange("(n p) c -> p n c", p=P))\
                            .then_inc(x_loaded, 16)
                sp.dma_start(wv[:], w_v).then_inc(wv_loaded, 16)
                if bo is not None:
                    sp.dma_start(bo_row[:], bo.rearrange("(a c) -> a c", a=1)).then_inc(bo_loaded, 16)

            @block.gpsimd
            def _(pool):
                if x_in is not None:
                    nc.gpsimd.memset(core.ident[:], 0.0).then_inc(const_step, 1)
                    nc.gpsimd.memset(core.ones_row[:], 1.0).then_inc(const_step, 1)
                    pool.wait_ge(const_step, 2)
                    nc.gpsimd.affine_select(out=core.ident[:], in_=core.ident[:], compare_op=ALU.not_equal,
                                            fill=1.0, base=0, pattern=[[-1, P]], channel_multiplier=1)\
                        .then_inc(const_ready, 1)
                table = att.rel if att.alibi else att.bias[0]
                if att.alibi:
                    for h in range(att.nq * KVH):
                        nc.gpsimd.memset(att.slopes[:, h:h + 1], float(slopes[h]))
                    nc.gpsimd.iota(table[:], pattern=[[8, SEQ]], base=-8 * (SEQ - P), channel_multiplier=-8,
                                   allow_small_or_imprecise_dtypes=True).then_inc(const_step, 1)
                else:
                    nc.gpsimd.memset(table[:], 0.0).then_inc(const_step, 1)
                pool.wait_ge(const_step, 3 if x_in is not None else 1)
                nc.gpsimd.affine_select(out=table[:], in_=table[:], compare_op=ALU.is_ge, fill=MASKED,
                                        base=SEQ - P, pattern=[[-1, SEQ]], channel_multiplier=1)

            @block.vector
            def _(dve):
                if x_in is not None:
                    dve.wait_ge(x_loaded, 64)
                norm.vector(dve, att.xh, att.xl)
                dve.wait_ge(wv_hi, 1)
                nc.vector.tensor_tensor(wvl[:], wv[:], wvh[:].bitcast(F32), ALU.subtract).then_inc(wv_lo, 1)
                for t in range(NT):
                    dve.wait_ge(v_done, t + 1)
                    nc.vector.tensor_copy(att.V[:, t, 512:1024], core.S[t % 2][:, 512:1024]).then_inc(v_dve, 1)
                if bo is not None:
                    dve.wait_ge(bo_wide, 1)
                    nc.vector.tensor_tensor(core.x[:], core.x[:],
                                            core.PJ[:, 0:C].unsqueeze(1).broadcast_to([P, NT, C]), ALU.add)

            @block.scalar
            def _(act):
                norm.scalar(act, att.xh)
                act.wait_ge(wv_loaded, 16)
                nc.scalar.activation(wvh[:], wv[:], ACT.Copy).then_inc(wv_hi, 1)
                for t in range(NT):
                    act.wait_ge(v_done, t + 1)
                    nc.scalar.activation(att.V[:, t, 0:512], core.S[t % 2][:, 0:512], ACT.Copy).then_inc(v_act, 1)

            @block.tensor
            def _(pe):
                if x_in is not None:
                    pe.wait_ge(const_ready, 1)
                norm.tensor(pe)
                if bo is not None:
                    pe.wait_ge(bo_loaded, 16)
                    nc.tensor.matmul(core.PJ[:, 0:C], core.ones_row[:], bo_row[:], start=True, stop=True)\
                        .then_inc(bo_wide, 1)
                pe.wait_ge(norm.split, norm.STEPS)
                pe.wait_ge(wv_lo, 1)
                for t in range(NT):
                    if t >= 2:
                        pe.wait_ge(v_act, t - 1)
                        pe.wait_ge(v_dve, t - 1)
                    xh, xl = att.xh[:, t * P:(t + 1) * P], att.xl[:, t * P:(t + 1) * P]
                    for half in range(2):
                        cols = slice(512 * half, 512 * half + 512)
                        out = core.S[t % 2][:, cols]
                        nc.tensor.matmul(out, xh, wvh[:, cols], start=True, stop=False)
                        nc.tensor.matmul(out, xh, wvl[:, cols], start=False, stop=False)
                        mm = nc.tensor.matmul(out, xl, wvh[:, cols], start=False, stop=True)
                    mm.then_inc(v_done, 1)

        with ExitStack() as c2:
            att.loop_memory(c2)
            block = c2.enter_context(nc.Block())

            @block.sync
            def _(sp):
                att.sync(sp)

            @block.gpsimd
            def _(pool):
                att.gpsimd(pool)

            @block.scalar
            def _(act):
                att.scalar(act)

            @block.vector
            def _(dve):
                att.vector(dve)

            @block.tensor
            def _(pe):
                att.tensor(pe)


def feed_forward(core, w_gate, w_up, w_down):
    nc = core.nc
    NF = FH // P
    SCALE = float(np.float32(1.0 / 127.0))
    with ExitStack() as ctx:
        norm = Norm(core, ctx, "ffn_norm", exact=True)

        def sb(n, shape, dt=F32):
            return ctx.enter_context(nc.sbuf_tensor(f"ffn_{n}", shape, dt))

        def sem(n):
            return ctx.enter_context(nc.semaphore(f"ffn_{n}"))

        w_int = [sb(f"w_int{k}", [P, NF, P], I32) for k in range(3)]
        w_f = [sb(f"w_f{k}", [P, NF, P]) for k in range(3)]
        w_T = [sb(f"w_T{k}", [P, NF, P]) for k in range(3)]
        silu = [sb(f"silu{k}", [P, 512]) for k in range(2)]
        h = [sb(f"h{k}", [P, NF, 512]) for k in range(2)]
        loaded, dequant, turned, copied = sem("loaded"), sem("dequant"), sem("turned"), sem("copied")
        gated, upped, silued, hidden = sem("gated"), sem("upped"), sem("silued"), sem("hidden")
        downed, added = sem("downed"), sem("added")
        block = ctx.enter_context(nc.Block())

        @block.sync
        def _(sp):
            for k, w in enumerate((w_gate, w_up)):
                sp.dma_start(w_int[k][:], w.rearrange("(n f) c -> f n c", f=P)).then_inc(loaded, 16)
            sp.dma_start(w_int[2][:], w_down.rearrange("c (n f) -> c n f", f=P)).then_inc(loaded, 16)

        @block.gpsimd
        def _(pool):
            pool.wait_ge(loaded, 48)
            for k in range(3):
                nc.gpsimd.tensor_scalar(w_f[k][:], w_int[k][:], SCALE, None, ALU.mult).then_inc(dequant, 1)

        @block.tensor
        def _(pe):
            for k in range(3):
                pe.wait_ge(dequant, k + 1)
                for n in range(NF):
                    mm = nc.tensor.transpose(core.S[k % 2][:, (512 * (k // 2)) + n * P:(512 * (k // 2)) + (n + 1) * P],
                                             w_f[k][:, n, :], core.ident[:])
                mm.then_inc(turned, 1)
            norm.tensor(pe)
            pe.wait_ge(copied, 3)

            def down(c):
                pe.wait_ge(hidden, NF * (c + 1))
                if c >= 1:
                    pe.wait_ge(added, c)
                for k in range(4):
                    for f in range(NF):
                        mm = nc.tensor.matmul(core.O[:, k * C:(k + 1) * C], h[c % 2][:, f, k * P:(k + 1) * P],
                                              w_T[2][:, f, :], start=(f == 0), stop=(f == NF - 1))
                mm.then_inc(downed, 1)

            for c in range(4):
                pe.wait_ge(norm.rounded, c + 1)
                for f in range(NF):
                    u = c * NF + f
                    x = norm.xT[:, c * 512:(c + 1) * 512]
                    if u >= 2:
                        pe.wait_ge(silued, u - 1)
                        pe.wait_ge(hidden, u - 1)
                    nc.tensor.matmul(core.S[u % 2][:, 0:512], w_T[0][:, f, :], x, start=True, stop=True)\
                        .then_inc(gated, 1)
                    nc.tensor.matmul(core.S[u % 2][:, 512:1024], w_T[1][:, f, :], x, start=True, stop=True)\
                        .then_inc(upped, 1)
                if c >= 1:
                    down(c - 1)
            down(3)

        @block.scalar
        def _(act):
            for k in range(3):
                act.wait_ge(turned, k + 1)
                o = 512 * (k // 2)
                nc.scalar.activation(w_T[k][:], core.S[k % 2][:, o:o + FH].rearrange("p (n c) -> p n c", c=P),
                                     ACT.Copy).then_inc(copied, 1)
            norm.scalar(act)
            for u in range(4 * NF):
                act.wait_ge(gated, u + 1)
                if u >= 2:
                    act.wait_ge(hidden, u - 1)
                nc.scalar.activation(silu[u % 2][:], core.S[u % 2][:, 0:512], ACT.Silu).then_inc(silued, 1)

        @block.vector
        def _(dve):
            norm.vector(dve)

            def add(c):
                dve.wait_ge(downed, c + 1)
                x = core.x[:, 4 * c:4 * c + 4, :]
                nc.vector.tensor_tensor(x, core.O[:].rearrange("p (n c) -> p n c", c=C), x, ALU.add)\
                    .then_inc(added, 1)

            for c in range(4):
                for f in range(NF):
                    u = c * NF + f
                    dve.wait_ge(silued, u + 1)
                    dve.wait_ge(upped, u + 1)
                    if c >= 2:
                        dve.wait_ge(downed, c - 1)
                    nc.vector.tensor_tensor(h[c % 2][:, f, :], core.S[u % 2][:, 512:1024], silu[u % 2][:],
                                            ALU.mult).then_inc(hidden, 1)
                if c >= 1:
                    add(c - 1)
            add(3)


def mixture(core, gate_w, w1, b1, w2, b2):
    nc = core.nc
    with ExitStack() as ctx:
        norm = Norm(core, ctx, "moe_norm", exact=True)

        def sb(n, shape, dt=F32):
            return ctx.enter_context(nc.sbuf_tensor(f"moe_{n}", shape, dt))

        factor = sb("factor", [P, NT, E])
        any_kept = sb("any_kept", [1, 1], I32)

        with ExitStack() as c1:
            def sb1(n, shape, dt=F32):
                return c1.enter_context(nc.sbuf_tensor(f"gate_{n}", shape, dt))

            def sem(n):
                return c1.enter_context(nc.semaphore(f"gate_{n}"))

            gw, gwT = sb1("gw", [E, C]), sb1("gwT", [C, E])
            ones = sb1("ones", [P, P])
            order = sb1("order", [P, E])
            probs, left, score = (sb1(n, [P, NT, E]) for n in ("probs", "left", "score"))
            first, second = sb1("first", [P, NT, E]), sb1("second", [P, NT, E])
            most, total = sb1("most", [P, NT]), sb1("total", [P, NT])
            count, keep = sb1("count", [P, E]), sb1("keep", [P, E])
            loaded, consts, gw_turned, gw_copied = sem("loaded"), sem("consts"), sem("gw_turned"), sem("gw_copied")
            logits_done, shifted, exped = sem("logits_done"), sem("shifted"), sem("exped")
            counted, summed, dve_done = sem("counted"), sem("summed"), sem("dve_done")
            block = c1.enter_context(nc.Block())

            @block.sync
            def _(sp):
                sp.dma_start(gw[:], gate_w).then_inc(loaded, 16)

            @block.gpsimd
            def _(pool):
                nc.gpsimd.memset(ones[:], 1.0).then_inc(consts, 1)
                nc.gpsimd.iota(order[:], pattern=[[-1, E]], base=E, channel_multiplier=0,
                               allow_small_or_imprecise_dtypes=True).then_inc(consts, 1)

            @block.tensor
            def _(pe):
                pe.wait_ge(loaded, 16)
                nc.tensor.transpose(core.PJ[:, 0:E], gw[:], core.ident[0:E, 0:E]).then_inc(gw_turned, 1)
                norm.tensor(pe)
                pe.wait_ge(gw_copied, 1)
                pe.wait_ge(norm.rounded, norm.STEPS)
                for t in range(NT):
                    mm = nc.tensor.matmul(core.PJ[:, t * E:(t + 1) * E], norm.xT[:, t * P:(t + 1) * P], gwT[:],
                                          start=True, stop=True)
                mm.then_inc(logits_done, 1)
                pe.wait_ge(consts, 2)
                pe.wait_ge(counted, 1)
                nc.tensor.matmul(core.O[:, 0:E], ones[:], count[:], start=True, stop=True).then_inc(summed, 1)

            @block.scalar
            def _(act):
                act.wait_ge(gw_turned, 1)
                nc.scalar.activation(gwT[:], core.PJ[:, 0:E], ACT.Copy).then_inc(gw_copied, 1)
                norm.scalar(act)
                act.wait_ge(shifted, 1)
                nc.scalar.activation(probs[:], left[:], ACT.Exp).then_inc(exped, 1)

            @block.vector
            def _(dve):
                norm.vector(dve)
                n = [0]

                def then(ins):
                    n[0] += 1
                    ins.then_inc(dve_done, 1)
                    dve.wait_ge(dve_done, n[0])

                def by_row(ap):
                    return ap.unsqueeze(2).broadcast_to([P, NT, E])

                def by_expert(ap):
                    return ap.unsqueeze(1).broadcast_to([P, NT, E])

                logits = core.PJ[:, 0:NT * E].rearrange("p (n e) -> p n e", e=E)
                dve.wait_ge(logits_done, 1)
                then(nc.vector.reduce_max(most[:], logits, AX.X))
                nc.vector.tensor_tensor(left[:], logits, by_row(most[:]), ALU.subtract).then_inc(shifted, 1)
                dve.wait_ge(exped, 1)
                then(nc.vector.reduce_sum(total[:], probs[:], AX.X))
                then(nc.vector.reciprocal(total[:], total[:]))
                then(nc.vector.tensor_tensor(probs[:], probs[:], by_row(total[:]), ALU.mult))
                dve.wait_ge(consts, 2)

                def top(p, out):
                    then(nc.vector.reduce_max(most[:], p[:], AX.X))
                    then(nc.vector.tensor_tensor(score[:], p[:], by_row(most[:]), ALU.is_equal))
                    then(nc.vector.tensor_tensor(score[:], score[:], by_expert(order[:]), ALU.mult))
                    then(nc.vector.reduce_max(most[:], score[:], AX.X))
                    then(nc.vector.tensor_tensor(out[:], score[:], by_row(most[:]), ALU.is_equal))

                top(probs, first)
                then(nc.vector.scalar_tensor_tensor(out=left[:], in0=first[:], scalar=-2.0, in1=probs[:],
                                                    op0=ALU.mult, op1=ALU.add))
                top(left, second)
                then(nc.vector.tensor_tensor(first[:], first[:], second[:], ALU.add))
                nc.vector.reduce_sum(count[:], first[:].rearrange("p n e -> p e n"), AX.X).then_inc(counted, 1)
                then(nc.vector.tensor_tensor(probs[:], probs[:], first[:], ALU.mult))
                dve.wait_ge(summed, 1)
                then(nc.vector.tensor_scalar(keep[:], core.O[:, 0:E], float(CAP), None, ALU.is_le))
                then(nc.vector.tensor_tensor(factor[:], probs[:], by_expert(keep[:]), ALU.mult))
                then(nc.vector.reduce_max(any_kept[:], keep[0:1, :], AX.X))

        experts(core, norm.xT, factor, any_kept, w1, b1, w2, b2)


def experts(core, xT, factor, any_kept, w1, b1, w2, b2):
    nc = core.nc
    CH = 4
    with ExitStack() as ctx:
        def sb(n, shape, dt=F32):
            return ctx.enter_context(nc.sbuf_tensor(f"exp_{n}", shape, dt))

        def sem(n):
            return ctx.enter_context(nc.semaphore(f"exp_{n}"))

        w = [sb("w1", [P, P]), sb("w2", [P, P])]
        wT = [sb("w1T", [P, P]), sb("w2T", [P, P])]
        b1_col, b2_row = sb("b1", [P, 1]), sb("b2", [1, P])
        h = [sb("h0", [P, 512]), sb("h1", [P, 512])]
        loaded, turned, copied = sem("loaded"), sem("turned"), sem("copied")
        upped, silued, downed, added = sem("upped"), sem("silued"), sem("downed"), sem("added")
        out_bank = [core.O, core.PJ]
        block = ctx.enter_context(nc.Block())

        @block.sync
        def _(sp):
            kept = sp.value_load(any_kept[0:1, 0:1], min_val=0, max_val=1)
            with sp.If(kept > 0):
                def load(e):
                    wait(sp, downed, e * CH)
                    one = bass.ds(e, 1)
                    sp.dma_start(w[0][:], w1[one, :, :].rearrange("e f c -> (e f) c")).then_inc(loaded, 16)
                    sp.dma_start(w[1][:], w2[one, :, :].rearrange("e g f -> (e g) f")).then_inc(loaded, 16)
                    sp.dma_start(b1_col[:], b1[one, :].rearrange("e f -> f e")).then_inc(loaded, 16)
                    sp.dma_start(b2_row[:], b2[one, :]).then_inc(loaded, 16)

                load(0)
                with sp.Fori(1, E) as e:
                    load(e)

        @block.tensor
        def _(pe):
            kept = pe.value_load(any_kept[0:1, 0:1], min_val=0, max_val=1)
            with pe.If(kept > 0):
                def expert(e):
                    wait(pe, loaded, (e + 1) * 64)
                    for k in range(2):
                        mm = nc.tensor.transpose(core.TP[k][:, 0:P], w[k][:], core.ident[:])
                    mm.then_inc(turned, 1)
                    wait(pe, copied, e + 1)

                    def down(c):
                        wait(pe, silued, e * CH + (c + 1))
                        wait(pe, added, e * CH + (c - 1))
                        for k in range(4):
                            out = out_bank[c % 2][:, k * P:(k + 1) * P]
                            nc.tensor.matmul(out, h[c % 2][:, k * P:(k + 1) * P], wT[1][:], start=True, stop=False)
                            mm = nc.tensor.matmul(out, core.ones_row[:], b2_row[:], start=False, stop=True)
                        mm.then_inc(downed, 1)

                    for c in range(CH):
                        wait(pe, silued, e * CH + (c - 1))
                        nc.tensor.matmul(core.S[c % 2][:, 0:512], wT[0][:], xT[:, c * 512:(c + 1) * 512],
                                         start=True, stop=True).then_inc(upped, 1)
                        if c >= 1:
                            down(c - 1)
                    down(CH - 1)

                expert(0)
                with pe.Fori(1, E) as e:
                    expert(e)

        @block.scalar
        def _(act):
            kept = act.value_load(any_kept[0:1, 0:1], min_val=0, max_val=1)
            with act.If(kept > 0):
                def expert(e):
                    wait(act, turned, e + 1)
                    wait(act, downed, e * CH)
                    for k in range(2):
                        last = nc.scalar.activation(wT[k][:], core.TP[k][:, 0:P], ACT.Copy)
                    last.then_inc(copied, 1)
                    for c in range(CH):
                        wait(act, upped, e * CH + (c + 1))
                        wait(act, downed, e * CH + (c - 1))
                        nc.scalar.activation(h[c % 2][:], core.S[c % 2][:, 0:512], ACT.Silu, bias=b1_col[:, 0:1])\
                            .then_inc(silued, 1)

                expert(0)
                with act.Fori(1, E) as e:
                    expert(e)

        @block.vector
        def _(dve):
            kept = dve.value_load(any_kept[0:1, 0:1], min_val=0, max_val=1)
            with dve.If(kept > 0):
                def expert(e):
                    for c in range(CH):
                        wait(dve, downed, e * CH + (c + 1))
                        wait(dve, added, e * CH + c)
                        for k in range(4):
                            t = 4 * c + k
                            last = nc.vector.scalar_tensor_tensor(
                                out=core.x[:, t, :], in0=out_bank[c % 2][:, k * P:(k + 1) * P],
                                scalar=factor[:, t, bass.ds(e, 1)], in1=core.x[:, t, :], op0=ALU.mult, op1=ALU.add)
                        last.then_inc(added, 1)

                expert(0)
                with dve.Fori(1, E) as e:
                    expert(e)


def store(core, out):
    nc = core.nc
    with nc.semaphore("stored") as stored, nc.Block() as block:
        @block.sync
        def _(sp):
            sp.dma_start(out.rearrange("(n p) c -> p n c", p=P), core.x[:]).then_inc(stored, 16)
            sp.wait_ge(stored, 16)


def program(nc, inputs, out):
    with ExitStack() as ctx:
        core = Core(nc, ctx)
        a = inputs
        w0 = a["L0_attn_W_qkv"]
        nq0 = 2 * KVH * D
        attention_layer(core, "a0", 2, w0[:, 0:nq0], w0[:, nq0:nq0 + KVH * D], w0[:, nq0 + KVH * D:],
                        a["L0_attn_W_out"], alibi_slopes(2 * KVH),
                        x_in=a["L0_attn_inputs"].rearrange("b s c -> (b s) c"))
        feed_forward(core, a["L0_ffn_w_gate"], a["L0_ffn_w_up"], a["L0_ffn_w_down"])
        attention_layer(core, "a1", 1, a["L1_attn_Wq"], a["L1_attn_Wk"], a["L1_attn_Wv"], a["L1_attn_Wo"],
                        None, bo=a["L1_attn_bo"])
        mixture(core, a["L1_ffn_gate_w"], a["L1_ffn_w1"], a["L1_ffn_b1"], a["L1_ffn_w2"], a["L1_ffn_b2"])
        store(core, out.rearrange("b s c -> (b s) c"))


_INS = ['L0_attn_inputs', 'L0_attn_W_qkv', 'L0_attn_W_out', 'L0_ffn_w_gate', 'L0_ffn_w_up', 'L0_ffn_w_down',
        'L1_attn_Wq', 'L1_attn_Wk', 'L1_attn_Wv', 'L1_attn_Wo', 'L1_attn_bo',
        'L1_ffn_gate_w', 'L1_ffn_w1', 'L1_ffn_b1', 'L1_ffn_w2', 'L1_ffn_b2']


def kernel(**inputs):
    import concourse.bacc as bacc
    from concourse.bass_utils import run_bass_kernel_spmd

    nc = bacc.Bacc("TRN2", target_bir_lowering=False, num_devices=1,
                   dynamic_dma_scratch_size=1024)
    arrays, aps = {}, {}
    for name in _INS:
        a = np.ascontiguousarray(inputs[name])
        arrays[name] = a
        aps[name] = nc.dram_tensor(name, a.shape, mybir.dt.from_np(a.dtype), kind="ExternalInput").ap()
    out = nc.dram_tensor("out", (BATCH, SEQ, C), F32, kind="ExternalOutput").ap()
    program(nc, aps, out)
    r = run_bass_kernel_spmd(nc, [arrays], core_ids=[0])
    return r.results[0]["out"]
```

```python
import numpy as np
import concourse.bass as bass
from concourse import mybir
from contextlib import ExitStack

F32 = mybir.dt.float32
F32R = mybir.dt.float32r
I32 = mybir.dt.int32
ALU = mybir.AluOpType
ACT = mybir.ActivationFunctionType
AX = mybir.AxisListType

P = 128
C = 128
BATCH = 2
SEQ = 1024
TOK = BATCH * SEQ
NT = TOK // P
QT = SEQ // P
D = 64
KVH = 16
FH = 384
E = 8
SCORE_BANKS = [[0], [1], [0], [2], [0, 1], [1, 2], [0, 1], [1, 2]]
LAG = 3
CAP = int(1.25 * TOK / E)
EPS = 1e-5
MASKED = -1e34
LANES = 4


def alibi_slopes(n):
    base = 2.0 ** (-2.0 ** (-(np.log2(n) - 3)))
    return (base ** np.arange(1, n + 1, dtype=np.float32)).astype(np.float32)


class Core:

    def __init__(self, nc, ctx):
        self.nc = nc

        def sb(name, shape, dt=F32):
            return ctx.enter_context(nc.sbuf_tensor(name, shape, dt))

        def ps(name, cols):
            return ctx.enter_context(nc.psum_tensor(name, [P, cols], F32))

        self.x = sb("x", [P, NT, C])
        self.ident = sb("ident", [P, P])
        self.ones_row = sb("ones_row", [1, P])
        self.scores = ps("scores", 2048)
        self.S = [self.scores[:, 0:1024], self.scores[:, 1024:2048]]
        self.TP = [ps("TP0", 512), ps("TP1", 512), self.scores[:, 1536:2048]]
        self.O = ps("O", 512)
        self.PJ = ps("PJ", 512)


def wait_apart(eng, sem, value, passed):
    wait(eng, sem, value)
    if not isinstance(value, int):
        eng.sem_inc(passed, 1)


def wait(eng, sem, value):
    if isinstance(value, int) and value <= 0:
        return
    eng.wait_ge(sem, value)


class Norm:

    def __init__(self, core, ctx, name, exact):
        nc = core.nc
        self.core, self.exact = core, exact

        def sb(n, shape, dt=F32):
            return ctx.enter_context(nc.sbuf_tensor(f"{name}_{n}", shape, dt))

        def sem(n):
            return ctx.enter_context(nc.semaphore(f"{name}_{n}"))

        self.xn = sb("xn", [P, NT, C])
        self.sum = sb("sum", [P, NT])
        self.neg_mean = sb("neg_mean", [P, NT])
        self.squares = sb("squares", [P, NT])
        self.var = sb("var", [P, NT])
        self.std = sb("std", [P, NT])
        self.rstd = sb("rstd", [P, NT])
        self.tmp = sb("tmp", [P, NT])
        if exact:
            self.xT = sb("xT", [P, TOK])
        self.summed = sem("summed")
        self.mean_ready = sem("mean_ready")
        self.squared = sem("squared")
        self.dve_done = sem("dve_done")
        self.var_ready = sem("var_ready")
        self.std_ready = sem("std_ready")
        self.xn_ready = sem("xn_ready")
        self.turned = sem("turned")
        self.rounded = sem("rounded")
        self.split = sem("split")

    STEPS = NT // LANES

    def vector(self, dve, hi=None, lo=None, loaded=None):
        nc, x = self.core.nc, self.core.x
        n = [0]

        def then(ins):
            n[0] += 1
            ins.then_inc(self.dve_done, 1)
            dve.wait_ge(self.dve_done, n[0])

        for g in range(self.STEPS + 1):
            if g < self.STEPS:
                s = slice(g * LANES, (g + 1) * LANES)
                if loaded is not None:
                    dve.wait_ge(loaded[g], 16)
                nc.vector.reduce_sum(self.sum[:, s], x[:, s, :], axis=AX.X).then_inc(self.summed, 1)
            if g >= 1:
                s = slice((g - 1) * LANES, g * LANES)
                dve.wait_ge(self.summed, g)
                nc.vector.tensor_scalar(self.neg_mean[:, s], self.sum[:, s], -1.0 / C, None, ALU.mult)\
                    .then_inc(self.mean_ready, 1)

        def var(half):
            s = slice(half * NT // 2, (half + 1) * NT // 2)
            dve.wait_ge(self.squared, (half + 1) * self.STEPS // 2)
            nc.vector.tensor_scalar(self.var[:, s], self.squares[:, s], 1.0 / C, EPS, ALU.mult, ALU.add)\
                .then_inc(self.var_ready, 1)

        def scale(half):
            s = slice(half * NT // 2, (half + 1) * NT // 2)
            dve.wait_ge(self.std_ready, half + 1)
            then(nc.vector.reciprocal(self.rstd[:, s], self.std[:, s]))
            then(nc.vector.tensor_tensor(self.tmp[:, s], self.rstd[:, s], self.rstd[:, s], ALU.mult))
            then(nc.vector.tensor_tensor(self.tmp[:, s], self.tmp[:, s], self.var[:, s], ALU.mult))
            then(nc.vector.tensor_scalar(self.tmp[:, s], self.tmp[:, s], -0.5, 1.5, ALU.mult, ALU.add))
            then(nc.vector.tensor_tensor(self.rstd[:, s], self.rstd[:, s], self.tmp[:, s], ALU.mult))
            if half == 0:
                var(1)
            for t in range(s.start, s.stop):
                tile = nc.vector.tensor_scalar(self.xn[:, t, :], x[:, t, :], self.neg_mean[:, t:t + 1],
                                               self.rstd[:, t:t + 1], ALU.add, ALU.mult)
                if t % LANES == LANES - 1:
                    tile.then_inc(self.xn_ready, 1)

        def rest(g):
            cols = slice(g * 512, (g + 1) * 512)
            dve.wait_ge(self.rounded, g + 1)
            nc.vector.tensor_tensor(lo[:, cols], self.core.TP[g % 2][:], hi[:, cols].bitcast(F32),
                                    ALU.subtract).then_inc(self.split, 1)

        var(0)
        for half in range(2):
            scale(half)
            if not self.exact:
                rest(2 * half)
                rest(2 * half + 1)

    def scalar(self, act):
        nc = self.core.nc

        def sqrt(half):
            s = slice(half * NT // 2, (half + 1) * NT // 2)
            act.wait_ge(self.var_ready, half + 1)
            nc.scalar.activation(self.std[:, s], self.var[:, s], ACT.Sqrt).then_inc(self.std_ready, 1)

        for g in range(self.STEPS):
            act.wait_ge(self.mean_ready, g + 1)
            for t in range(g * LANES, (g + 1) * LANES):
                tile = nc.scalar.activation(self.xn[:, t, :], self.core.x[:, t, :], ACT.Square,
                                            bias=self.neg_mean[:, t:t + 1], accum_out=self.squares[:, t:t + 1])
            tile.then_inc(self.squared, 1)
            if g == self.STEPS // 2:
                sqrt(0)
        sqrt(1)

    def round(self, act, hi=None):
        nc = self.core.nc
        for g in range(self.STEPS):
            act.wait_ge(self.turned, g + 1)
            out = self.xT if self.exact else hi
            nc.scalar.activation(out[:, g * 512:(g + 1) * 512], self.core.TP[g % 2][:], ACT.Copy)\
                .then_inc(self.rounded, 1)

    def tensor(self, pe, steps=range(NT // LANES)):
        nc = self.core.nc
        for g in steps:
            pe.wait_ge(self.xn_ready, g + 1)
            if g >= 2:
                pe.wait_ge(self.rounded if self.exact else self.split, g - 1)
            for n in range(LANES):
                last = nc.tensor.transpose(self.core.TP[g % 2][:, n * P:(n + 1) * P],
                                           self.xn[:, g * LANES + n, :], self.core.ident[:])
            last.then_inc(self.turned, 1)


class Attention:

    def __init__(self, core, ctx, name, nq, w_q, w_k, w_out, slopes):
        nc = core.nc
        self.core, self.nq, self.name = core, nq, name
        self.w_q, self.w_k, self.w_out = w_q, w_k, w_out
        self.alibi = slopes is not None
        self.n = 2 * nq * QT
        self.groups = self.n // 4
        self.chunks = 12 * self.n // QT
        self.parts = 1 + nq
        self.proj = 2 * self.parts
        self.when = {2: [0, 3, 5, 8, 11, 13], 1: [0, 2, 3, 5]}[nq]
        self.weights_step = self.when[-1]

        def sb(n, shape, dt=F32):
            return ctx.enter_context(nc.sbuf_tensor(f"{name}_{n}", shape, dt))

        def sem(n):
            return ctx.enter_context(nc.semaphore(f"{name}_{n}"))

        self.xh = sb("xh", [P, TOK], F32R)
        self.xl = sb("xl", [P, TOK], F32R)
        self.V = sb("V", [P, NT, KVH * D])
        if self.alibi:
            self.rel = sb("rel", [P, SEQ])
            self.slopes = sb("slopes", [P, nq * KVH])
            self.slope = sb("slope", [P, nq])
        self.bias = [sb(f"bias{h}", [P, SEQ]) for h in range(nq if self.alibi else 1)]
        self.raw_qk = sb("raw_qk", [P, self.parts, D])
        self.raw_out = sb("raw_out", [P, nq, C])
        self.w_proj = sb("w_proj", [P, self.parts, 2, 2, D], F32R)
        self.w_o = sb("w_o", [P, nq, C])

        self.qk_loaded = sem("qk_loaded")
        self.out_loaded = sem("out_loaded")
        self.w_hi = sem("w_hi")
        self.w_lo = sem("w_lo")
        self.w_o_ready = sem("w_o_ready")
        self.v_hi = sem("v_hi")
        self.v_lo = sem("v_lo")
        self.bias_ready = sem("bias_ready")
        self.slope_ready = sem("slope_ready")
        self.passed = sem("passed")
        self.pool_passed = sem("pool_passed")
        self.pj_done = sem("pj_done")
        self.pj_hi = sem("pj_hi")
        self.pj_lo = sem("pj_lo")
        self.scored = sem("scored")
        self.maxed = sem("maxed")
        self.exped = sem("exped")
        self.turned = sem("turned")
        self.p_hi = sem("p_hi")
        self.p_lo = sem("p_lo")
        self.valued = sem("valued")
        self.o_copied = sem("o_copied")
        self.out_done = sem("out_done")
        self.recip_done = sem("recip_done")
        self.added = sem("added")

    def loop_memory(self, ctx):
        nc, name, nq = self.core.nc, self.name, self.nq

        def sb(n, shape, dt=F32):
            return ctx.enter_context(nc.sbuf_tensor(f"{name}_{n}", shape, dt))

        self.KH = [sb(f"KH{b}", [P, SEQ], F32R) for b in range(2)]
        self.KL = [sb(f"KL{b}", [P, SEQ], F32R) for b in range(2)]
        self.Q = [[sb(f"Q{b}{h}", [P, SEQ], F32R) for h in range(nq)] for b in range(2)]
        self.VS = [sb(f"VS{b}", [P, QT, 2, D], F32R) for b in range(2)]
        self.prob = [sb(f"prob{i}", [P, SEQ]) for i in range(4)]
        self.neg_max = sb("neg_max", [P, 4])
        self.row_sum = sb("row_sum", [P, 16])
        self.recip = sb("recip", [P, 16])
        self.PH = [sb(f"PH{g}", [P, 4 * (g + 1), 512], F32R) for g in range(2)]
        self.PL = [sb(f"PL{g}", [P, 4 * (g + 1), 512], F32R) for g in range(2)]
        self.pj_copy = [sb(f"pj_copy{k}", [P, 512]) for k in range(2)]
        self.o_sb = [sb(f"o_sb{i}", [P, 512]) for i in range(2)]

    def place(self, s):
        s %= self.n
        return s // (self.nq * QT), (s // QT) % self.nq, s % QT

    def first_chunk(self, s):
        t = s % QT
        return (s // QT) * 12 + (t if t < 4 else 4 + 2 * (t - 4))

    def score_banks(self, s):
        return SCORE_BANKS[s % QT]

    def score_columns(self, s):
        first = min(self.score_banks(s)) * 512
        return self.core.scores[:, first:first + (s % QT + 1) * P]

    def bank_freed(self, s, bank):
        return max(k for k in range(s - 4, s) if bank in self.score_banks(k)) + 1

    def end_chunk(self, s):
        return self.first_chunk(s) + (1 if s % QT < 4 else 2)

    def at(self, i, per_turn, count):
        return i * per_turn + count

    def projections(self, s, last):
        half = self.n // 2
        phase, k = s // half, s % half
        if s >= self.n or (phase == 1 and last) or k not in self.when:
            return None
        return 1 - phase, self.when.index(k)

    def steps(self, first, last):
        for s in range(self.n + (LAG + 4 if last else 0)):
            def live(k):
                return k < self.n and (k >= 0 or not first)
            yield s, live

    def first_bank(self, m):
        return self.core.scores[:, (m % 3) * 512:(m % 3 + 1) * 512]

    def part_of(self, b, m):
        part, cols = m // 2, slice((m % 2) * 512, (m % 2) * 512 + 512)
        return part, cols

    def load(self, sp, j):
        w_q, w_k, w_out, nq = self.w_q, self.w_k, self.w_out, self.nq
        if not isinstance(j, int) or j > 0:
            sp.wait_ge(self.w_lo, j)
        sp.dma_start(self.raw_qk[:, 0, :], w_k[:, bass.ds(j * D, D)]).then_inc(self.qk_loaded, 16)
        sp.dma_start(self.raw_qk[:, 1:1 + nq, :],
                     w_q[:, bass.ds(j * (nq * D), nq * D)].rearrange("c (h d) -> c h d", d=D))\
            .then_inc(self.qk_loaded, 16)
        if not isinstance(j, int) or j > 0:
            sp.wait_ge(self.w_o_ready, j)
        rows = w_out[bass.ds(j * (nq * D), nq * D), :].rearrange("(h d) c -> d h c", d=D)
        for half in range(2):
            sp.dma_start(self.raw_out[half * D:(half + 1) * D, :, :], rows)\
                .then_inc(self.out_loaded, 16)

    def sync(self, sp):
        with sp.Fori(1, KVH) as j:
            self.load(sp, j)

    def pool_w_lo(self, pool, j, before):
        nc = self.core.nc
        wait(pool, *before)
        wait(pool, self.w_hi, j + 1)
        wait(pool, self.qk_loaded, (j + 1) * 32)
        for twice in range(2):
            last = nc.gpsimd.tensor_tensor(self.w_proj[:, :, 1, twice, :], self.raw_qk[:],
                                           self.w_proj[:, :, 0, twice, :].bitcast(F32), ALU.subtract)
        last.then_inc(self.w_lo, 1)
        return self.w_lo, j + 1

    def pool_bias(self, pool, j, h, freed, count, before):
        nc = self.core.nc
        wait(pool, *before)
        wait_apart(pool, self.maxed, freed, self.pool_passed)
        nc.gpsimd.tensor_copy(self.slope[:, h:h + 1], self.slopes[:, bass.ds(j * self.nq + h, 1)])\
            .then_inc(self.slope_ready, 1)
        wait_apart(pool, self.slope_ready, count, self.pool_passed)
        nc.gpsimd.tensor_tensor(self.bias[h][:], self.rel[:],
                                self.slope[:, h:h + 1].broadcast_to([P, SEQ]), ALU.mult)\
            .then_inc(self.bias_ready, 1)
        return self.bias_ready, count

    def gpsimd(self, pool):
        nc, n, nq = self.core.nc, self.n, self.nq
        PJ = 2 * self.proj

        def v_lo(j, b, count, before):
            wait(pool, *before)
            wait(pool, self.v_hi, count)
            nc.gpsimd.tensor_tensor(self.VS[b][:, :, 1, :], self.V[:, b * QT:(b + 1) * QT, bass.ds(j * D, D)],
                                    self.VS[b][:, :, 0, :].bitcast(F32), ALU.subtract).then_inc(self.v_lo, 1)
            return self.v_lo, count

        def w_o(j, freed, before):
            wait(pool, *before)
            wait(pool, self.out_loaded, (j + 1) * 32)
            wait_apart(pool, self.out_done, freed, self.pool_passed)
            nc.gpsimd.tensor_copy(self.w_o[:], self.raw_out[:]).then_inc(self.w_o_ready, 1)
            return self.w_o_ready, j + 1

        def project_lo(b, m, event, before):
            part, cols = self.part_of(b, m)
            wait(pool, *before)
            wait(pool, self.pj_hi, event + 1)
            if part == 0:
                hi, lo, rows = self.KH[b][:, cols], self.KL[b][:, cols], slice(0, P)
            else:
                hi = lo = self.Q[b][part - 1][D:P, cols]
                rows = slice(D, P)
            nc.gpsimd.tensor_tensor(lo, self.pj_copy[m % 2][rows, :], hi.bitcast(F32), ALU.subtract)\
                .then_inc(self.pj_lo, 1)
            return self.pj_lo, event + 1

        def turn(i, last, before):
            for s in range(n):
                if pj := self.projections(s, last):
                    phase = s // (n // 2)
                    before = project_lo(*pj, self.at(i, PJ, self.proj * (1 + phase) + pj[1]), before)
                if s == 1 and nq == 2:
                    before = self.pool_bias(pool, i, 1, self.at(i, n, 0), self.at(i, nq, 2), before)
                if s == 7:
                    before = w_o(i, self.at(i, self.groups, 0), before)
                if s == 6:
                    before = v_lo(i, 1, self.at(i, 2, 2), before)
                if last:
                    continue
                if s == self.weights_step:
                    before = self.pool_w_lo(pool, i + 1, before)
                if s == n // 2 + 6:
                    before = v_lo(i + 1, 0, self.at(i, 2, 3), before)
                if self.alibi and s == n - (nq - 1) * QT + 2:
                    before = self.pool_bias(pool, i + 1, 0, self.at(i, n, n - (nq - 1) * QT), self.at(i, nq, nq + 1), before)

        before = (self.pj_lo, 0)
        for m in range(self.proj):
            before = project_lo(0, m, m, before)
        before = v_lo(0, 0, 1, before)
        turn(0, False, before)

        def end_of_turn(i):
            late_projection = self.when[-1] > 6
            return (self.pj_lo, self.at(i, PJ, self.proj)) if late_projection else (self.v_lo, self.at(i, 2, 1))

        with pool.Fori(1, KVH - 1) as i:
            turn(i, False, end_of_turn(i))
        turn(KVH - 1, True, end_of_turn(KVH - 1))

    def act_w_hi(self, act, j, freed):
        nc = self.core.nc
        wait(act, self.qk_loaded, (j + 1) * 32)
        wait(act, self.pj_done, freed)
        for twice in range(2):
            last = nc.scalar.activation(self.w_proj[:, :, 0, twice, :], self.raw_qk[:], ACT.Copy)
        last.then_inc(self.w_hi, 1)

    def scalar(self, act):
        nc, n, nq = self.core.nc, self.n, self.nq
        G, CH, PJ = self.groups, self.chunks, 2 * self.proj

        def v_hi(j, b, freed):
            wait(act, self.valued, freed)
            nc.scalar.activation(self.VS[b][:, :, 0, :], self.V[:, b * QT:(b + 1) * QT, bass.ds(j * D, D)],
                                 ACT.Copy).then_inc(self.v_hi, 1)

        def project_hi(b, m, event, freed, bank=self.core.PJ):
            part, cols = self.part_of(b, m)
            wait(act, self.pj_done, event + 1)
            wait(act, self.scored, freed)
            out = self.KH[b] if part == 0 else self.Q[b][part - 1]
            nc.scalar.activation(out[:, cols], bank[:], ACT.Copy)
            wait(act, self.pj_lo, event - 1)
            rows = slice(0, P) if part == 0 else slice(D, P)
            nc.scalar.activation(self.pj_copy[m % 2][rows, :], bank[rows, :], ACT.Copy).then_inc(self.pj_hi, 1)

        def round_probs(i, e, c):
            b, h, t = self.place(e)
            g = t // 4
            wait(act, self.turned, self.at(i, CH, c + 1))
            if t % 4 == 0:
                wait(act, self.valued, self.at(i, G, e // 4 - 1))
            k0 = 4 * (c - self.first_chunk(e))
            nk = min(4, t + 1 - k0)
            nc.scalar.activation(self.PH[g][:, k0:k0 + nk, (t % 4) * P:(t % 4 + 1) * P],
                                 self.core.TP[c % 3][:, 0:nk * P].rearrange("p (k q) -> p k q", q=P),
                                 ACT.Copy).then_inc(self.p_hi, 1)

        def turn(i, first, last):
            for s, live in self.steps(first, last):
                if pj := self.projections(s, last):
                    phase = s // (n // 2)
                    project_hi(*pj, self.at(i, PJ, self.proj * (1 + phase) + pj[1]),
                               self.at(i, n, phase * (n // 2)))
                e = s - LAG - 4
                if e % 4 == 3 and live(e):
                    q = e // 4
                    wait(act, self.valued, self.at(i, G, q + 1))
                    wait(act, self.out_done, self.at(i, G, q - 1))
                    nc.scalar.activation(self.o_sb[q % 2][:], self.core.O[:], ACT.Copy).then_inc(self.o_copied, 1)
                if live(s - LAG - 1):
                    for c in range(self.first_chunk(s - LAG - 1) + 1, self.end_chunk(s - LAG - 1)):
                        round_probs(i, s - LAG - 1, c)
                if live(s - LAG):
                    round_probs(i, s - LAG, self.first_chunk(s - LAG))
                e = s - 1
                if live(e):
                    b, h, t = self.place(e)
                    nk = (t + 1) * P
                    wait(act, self.maxed, self.at(i, n, e + 1))
                    nc.scalar.activation(self.prob[e % 4][:, 0:nk], self.prob[e % 4][:, 0:nk], ACT.Exp,
                                         bias=self.neg_max[:, e % 4:e % 4 + 1], scale=-1.0,
                                         accum_out=self.row_sum[:, e % 16:e % 16 + 1]).then_inc(self.exped, 1)
                if s == 6:
                    v_hi(i, 1, self.at(i, G, 0))
                if s == self.weights_step and not last:
                    self.act_w_hi(act, i + 1, self.at(i, PJ, 2 * self.proj))
                if s == n // 2 + 6 and not last:
                    v_hi(i + 1, 0, self.at(i, G, G // 2))

        for m in range(self.proj):
            project_hi(0, m, m, 0, self.first_bank(m))
        v_hi(0, 0, 0)
        turn(0, True, False)
        with act.Fori(1, KVH - 1) as i:
            turn(i, False, False)
        turn(KVH - 1, False, True)

    def vector(self, dve):
        nc, n, nq = self.core.nc, self.n, self.nq
        G, CH, PJ = self.groups, self.chunks, 2 * self.proj

        def rest_of_probs(i, e, c):
            b, h, t = self.place(e)
            g = t // 4
            wait(dve, self.p_hi, self.at(i, CH, c + 1))
            k0 = 4 * (c - self.first_chunk(e))
            nk = min(4, t + 1 - k0)
            cols = slice((t % 4) * P, (t % 4 + 1) * P)
            nc.vector.tensor_tensor(self.PL[g][:, k0:k0 + nk, cols],
                                    self.core.TP[c % 3][:, 0:nk * P].rearrange("p (k q) -> p k q", q=P),
                                    self.PH[g][:, k0:k0 + nk, cols].bitcast(F32), ALU.subtract).then_inc(self.p_lo, 1)

        def turn(i, first, last):
            for s, live in self.steps(first, last):
                if s < n:
                    b, h, t = self.place(s)
                    nk = (t + 1) * P
                    if self.alibi and t == 0 and b == 0:
                        wait(dve, self.bias_ready, self.at(i, nq, h + 1))
                    wait(dve, self.turned, self.at(i, CH, self.end_chunk(s - 4)))
                    wait_apart(dve, self.scored, self.at(i, n, s + 1), self.passed)
                    nc.vector.tensor_tensor_reduce(
                        out=self.prob[s % 4][:, 0:nk], in0=self.score_columns(s),
                        in1=self.bias[h if self.alibi else 0][:, SEQ - nk:SEQ], scale=-1.0 / 8, scalar=3e38,
                        op0=ALU.add, op1=ALU.min, accum_out=self.neg_max[:, s % 4:s % 4 + 1]).then_inc(self.maxed, 1)
                if live(s - LAG):
                    rest_of_probs(i, s - LAG, self.first_chunk(s - LAG))
                e = s - LAG - 4
                if e % 4 == 3 and live(e):
                    q = e // 4
                    b, h, t = self.place(e)
                    r = 4 * (q % 4)
                    wait(dve, self.exped, self.at(i, n, e + 1))
                    nc.vector.reciprocal(self.recip[:, r:r + 4], self.row_sum[:, r:r + 4]).then_inc(self.recip_done, 1)
                    wait(dve, self.recip_done, self.at(i, G, q + 1))
                    wait(dve, self.out_done, self.at(i, G, q + 1))
                    wait(dve, self.added, self.at(i, G, q))
                    for k in range(4):
                        x = self.core.x[:, b * QT + t - 3 + k, :]
                        last_add = nc.vector.scalar_tensor_tensor(
                            out=x, in0=self.core.O[:, k * C:(k + 1) * C], scalar=self.recip[:, r + k:r + k + 1],
                            in1=x, op0=ALU.mult, op1=ALU.add)
                    last_add.then_inc(self.added, 1)
                if live(s - LAG):
                    for c in range(self.first_chunk(s - LAG) + 1, self.end_chunk(s - LAG)):
                        rest_of_probs(i, s - LAG, c)

        turn(0, True, False)
        with dve.Fori(1, KVH - 1) as i:
            turn(i, False, False)
        turn(KVH - 1, False, True)

    def tensor(self, pe):
        nc, n, nq = self.core.nc, self.n, self.nq
        G, CH, PJ = self.groups, self.chunks, 2 * self.proj

        def project(b, m, freed, weights, bank=self.core.PJ):
            part, cols = self.part_of(b, m)
            tok = slice(b * SEQ + cols.start, b * SEQ + cols.stop)
            if m == 0:
                wait(pe, self.w_lo, weights)
            wait(pe, self.pj_hi, freed)
            w = [self.w_proj[:, part, k, :, :].rearrange("c a d -> c (a d)") for k in range(2)]
            nc.tensor.matmul(bank[:], w[0], self.xh[:, tok], start=True, stop=False)
            nc.tensor.matmul(bank[:], w[1], self.xh[:, tok], start=False, stop=False)
            nc.tensor.matmul(bank[:], w[0], self.xl[:, tok], start=False, stop=True)\
                .then_inc(self.pj_done, 1)

        def turn_probs(i, e, c):
            b, h, t = self.place(e)
            wait(pe, self.exped, self.at(i, n, e + 1))
            wait(pe, self.p_lo, self.at(i, CH, c - 2))
            k0 = 4 * (c - self.first_chunk(e))
            for k in range(k0, min(k0 + 4, t + 1)):
                mm = nc.tensor.transpose(self.core.TP[c % 3][:, (k - k0) * P:(k - k0 + 1) * P],
                                         self.prob[e % 4][:, k * P:(k + 1) * P], self.core.ident[:])
            mm.then_inc(self.turned, 1)

        def scores(i, s):
            b, h, t = self.place(s)
            if t == 0:
                wait(pe, self.pj_lo, self.at(i, PJ, self.proj * (1 + b) - 2 * (nq - 1 - h)))
            q = self.Q[b][h][:, t * P:(t + 1) * P]
            for j in sorted(range(len(self.score_banks(s))),
                            key=lambda j: self.bank_freed(s, self.score_banks(s)[j])):
                wait(pe, self.maxed, self.at(i, n, self.bank_freed(s, self.score_banks(s)[j])))
                k0, k1 = j * 512, min((j + 1) * 512, (t + 1) * P)
                out = self.score_columns(s)[:, k0:k1]
                nc.tensor.matmul(out, q, self.KH[b][:, k0:k1], start=True, stop=False)
                mm = nc.tensor.matmul(out, q, self.KL[b][:, k0:k1], start=False, stop=True)
            mm.then_inc(self.scored, 1)

        def values(i, e, first_tile, end_tile):
            b, h, t = self.place(e)
            g, q = t // 4, e // 4
            if first_tile == 0:
                wait(pe, self.p_lo, self.at(i, CH, self.end_chunk(e)))
                wait(pe, self.added, self.at(i, G, q))
                if e % (n // 2) == 3:
                    wait(pe, self.v_lo, self.at(i, 2, 2 * (e // n) + 1 + b))
            for k in range(first_tile, end_tile):
                lo = max(0, k - 4 * g) * P
                v = self.VS[b][:, k, :, :].rearrange("k a d -> k (a d)")
                nc.tensor.matmul(self.core.O[:, lo:512], v, self.PH[g][:, k, lo:512],
                                 start=(k == 0), stop=False)
                mm = nc.tensor.matmul(self.core.O[:, lo:512], v, self.PL[g][:, k, lo:512],
                                      start=False, stop=(k == t))
            if end_tile == t + 1:
                mm.then_inc(self.valued, 1)

        def project_out(i, e):
            b, h, t = self.place(e)
            q = e // 4
            wait(pe, self.o_copied, self.at(i, G, q + 1))
            if e == 3:
                wait(pe, self.w_o_ready, self.at(i, 1, 1))
            for k in range(4):
                mm = nc.tensor.matmul(self.core.O[:, k * C:(k + 1) * C],
                                      self.o_sb[q % 2][:, k * P:(k + 1) * P], self.w_o[:, h, :],
                                      start=True, stop=True)
            mm.then_inc(self.out_done, 1)

        def turn(i, first, last):
            for s, live in self.steps(first, last):
                if pj := self.projections(s, last):
                    phase = s // (n // 2)
                    project(*pj, self.at(i, PJ, self.proj * (1 + phase) + pj[1]), self.at(i, 1, 1 + phase))
                e = s - LAG - 3
                if e % 4 == 3 and live(e):
                    values(i, e, 0, 4)
                e = s - LAG - 4
                if e % QT == QT - 1 and live(e):
                    values(i, e, 4, QT)
                if live(s - LAG - 1):
                    for c in range(self.first_chunk(s - LAG - 1) + 1, self.end_chunk(s - LAG - 1)):
                        turn_probs(i, s - LAG - 1, c)
                if live(s - LAG):
                    turn_probs(i, s - LAG, self.first_chunk(s - LAG))
                if first and s == 1:
                    wait(pe, self.pj_hi, self.proj)
                if s < n:
                    scores(i, s)
                e = s - LAG - 4
                if e % 4 == 3 and live(e):
                    project_out(i, e)

        for m in range(self.proj):
            project(0, m, m - 2, 1, self.first_bank(m))
        turn(0, True, False)
        with pe.Fori(1, KVH - 1) as i:
            turn(i, False, False)
        turn(KVH - 1, False, True)


def attention_layer(core, name, nq, w_q, w_k, w_v, w_out, slopes, x_in=None, bo=None):
    nc = core.nc
    with ExitStack() as ctx:
        att = Attention(core, ctx, name, nq, w_q, w_k, w_out, slopes)

        with ExitStack() as c1:
            norm = Norm(core, c1, name + "_norm", exact=False)
            wv = c1.enter_context(nc.sbuf_tensor(f"{name}_wv", [P, KVH * D], F32))
            wvh = c1.enter_context(nc.sbuf_tensor(f"{name}_wvh", [P, KVH * D], F32R))
            wvl = c1.enter_context(nc.sbuf_tensor(f"{name}_wvl", [P, KVH * D], F32R))
            bo_row = c1.enter_context(nc.sbuf_tensor(f"{name}_bo", [1, C], F32))

            def sem(n):
                return c1.enter_context(nc.semaphore(f"{name}_{n}"))
            x_loaded = None if x_in is None else [sem(f"x_loaded{g}") for g in range(norm.STEPS)]
            wv_loaded, bo_loaded = sem("wv_loaded"), sem("bo_loaded")
            wv_hi, wv_lo, const_ready, const_step = sem("wv_hi"), sem("wv_lo"), sem("const_ready"), sem("const_step")
            v_done, v_act, v_dve = sem("v_done"), sem("v_act"), sem("v_dve")
            bo_wide = sem("bo_wide")
            block = c1.enter_context(nc.Block())

            @block.sync
            def _(sp):
                if x_in is not None:
                    for g in range(4):
                        sp.dma_start(core.x[:, 4 * g:4 * g + 4, :],
                                     x_in[4 * g * P:4 * (g + 1) * P, :].rearrange("(n p) c -> p n c", p=P))\
                            .then_inc(x_loaded[g], 16)
                sp.dma_start(wv[:], w_v).then_inc(wv_loaded, 16)
                att.load(sp, 0)
                if bo is not None:
                    sp.dma_start(bo_row[:], bo.rearrange("(a c) -> a c", a=1)).then_inc(bo_loaded, 16)

            @block.gpsimd
            def _(pool):
                if x_in is not None:
                    nc.gpsimd.memset(core.ident[:], 0.0).then_inc(const_step, 1)
                    nc.gpsimd.memset(core.ones_row[:], 1.0).then_inc(const_step, 1)
                    pool.wait_ge(const_step, 2)
                    nc.gpsimd.affine_select(out=core.ident[:], in_=core.ident[:], compare_op=ALU.not_equal,
                                            fill=1.0, base=0, pattern=[[-1, P]], channel_multiplier=1)\
                        .then_inc(const_ready, 1)
                table = att.rel if att.alibi else att.bias[0]
                if att.alibi:
                    for h in range(att.nq * KVH):
                        nc.gpsimd.memset(att.slopes[:, h:h + 1], float(slopes[h]))
                    nc.gpsimd.iota(table[:], pattern=[[8, SEQ]], base=-8 * (SEQ - P), channel_multiplier=-8,
                                   allow_small_or_imprecise_dtypes=True).then_inc(const_step, 1)
                else:
                    nc.gpsimd.memset(table[:], 0.0).then_inc(const_step, 1)
                pool.wait_ge(const_step, 3 if x_in is not None else 1)
                nc.gpsimd.affine_select(out=table[:], in_=table[:], compare_op=ALU.is_ge, fill=MASKED,
                                        base=SEQ - P, pattern=[[-1, SEQ]], channel_multiplier=1)\
                    .then_inc(const_step, 1)
                pool.wait_ge(wv_loaded, 16)
                nc.gpsimd.tensor_copy(wvh[:], wv[:]).then_inc(wv_hi, 1)
                pool.wait_ge(wv_hi, 1)
                nc.gpsimd.tensor_tensor(wvl[:], wv[:], wvh[:].bitcast(F32), ALU.subtract).then_inc(wv_lo, 1)
                before = (wv_lo, 1)
                if att.alibi:
                    before = att.pool_bias(pool, 0, 0, 0, 1, before)
                att.pool_w_lo(pool, 0, before)

            @block.vector
            def _(dve):
                norm.vector(dve, att.xh, att.xl, x_loaded)
                for t in range(NT):
                    dve.wait_ge(v_done, t + 1)
                    nc.vector.tensor_copy(att.V[:, t, 512:1024], core.S[t % 2][:, 512:1024]).then_inc(v_dve, 1)
                if bo is not None:
                    dve.wait_ge(bo_wide, 1)
                    nc.vector.tensor_tensor(core.x[:], core.x[:],
                                            core.PJ[:, 0:C].unsqueeze(1).broadcast_to([P, NT, C]), ALU.add)

            @block.scalar
            def _(act):
                norm.scalar(act)
                norm.round(act, att.xh)
                act.wait_ge(wv_loaded, 16)
                att.act_w_hi(act, 0, 0)
                for t in range(NT):
                    act.wait_ge(v_done, t + 1)
                    nc.scalar.activation(att.V[:, t, 0:512], core.S[t % 2][:, 0:512], ACT.Copy).then_inc(v_act, 1)

            @block.tensor
            def _(pe):
                if x_in is not None:
                    pe.wait_ge(const_ready, 1)
                norm.tensor(pe, range(2))
                if bo is not None:
                    pe.wait_ge(bo_loaded, 16)
                    nc.tensor.matmul(core.PJ[:, 0:C], core.ones_row[:], bo_row[:], start=True, stop=True)\
                        .then_inc(bo_wide, 1)
                pe.wait_ge(wv_lo, 1)
                for t in range(NT):
                    if t == 2:
                        norm.tensor(pe, range(2, norm.STEPS))
                    if t % LANES == 0:
                        pe.wait_ge(norm.split, t // LANES + 1)
                    if t >= 2:
                        pe.wait_ge(v_act, t - 1)
                        pe.wait_ge(v_dve, t - 1)
                    xh, xl = att.xh[:, t * P:(t + 1) * P], att.xl[:, t * P:(t + 1) * P]
                    for half in range(2):
                        cols = slice(512 * half, 512 * half + 512)
                        out = core.S[t % 2][:, cols]
                        nc.tensor.matmul(out, xh, wvh[:, cols], start=True, stop=False)
                        nc.tensor.matmul(out, xh, wvl[:, cols], start=False, stop=False)
                        mm = nc.tensor.matmul(out, xl, wvh[:, cols], start=False, stop=True)
                    mm.then_inc(v_done, 1)

        with ExitStack() as c2:
            att.loop_memory(c2)
            block = c2.enter_context(nc.Block())

            @block.sync
            def _(sp):
                att.sync(sp)

            @block.gpsimd
            def _(pool):
                att.gpsimd(pool)

            @block.scalar
            def _(act):
                att.scalar(act)

            @block.vector
            def _(dve):
                att.vector(dve)

            @block.tensor
            def _(pe):
                att.tensor(pe)


def feed_forward(core, w_gate, w_up, w_down):
    nc = core.nc
    NF = FH // P
    SCALE = float(np.float32(1.0 / 127.0))
    with ExitStack() as ctx:
        norm = Norm(core, ctx, "ffn_norm", exact=True)

        def sb(n, shape, dt=F32):
            return ctx.enter_context(nc.sbuf_tensor(f"ffn_{n}", shape, dt))

        def sem(n):
            return ctx.enter_context(nc.semaphore(f"ffn_{n}"))

        w_int = [sb(f"w_int{k}", [P, NF, P], I32) for k in range(3)]
        w_f = [sb(f"w_f{k}", [P, NF, P]) for k in range(3)]
        w_T = [sb(f"w_T{k}", [P, NF, P]) for k in range(3)]
        silu = [sb(f"silu{k}", [P, 512]) for k in range(2)]
        h = [sb(f"h{k}", [P, NF, 512]) for k in range(2)]
        loaded, dequant, turned, copied = sem("loaded"), sem("dequant"), sem("turned"), sem("copied")
        gated, upped, silued, hidden = sem("gated"), sem("upped"), sem("silued"), sem("hidden")
        downed, added = sem("downed"), sem("added")
        block = ctx.enter_context(nc.Block())

        @block.sync
        def _(sp):
            for k, w in enumerate((w_gate, w_up)):
                sp.dma_start(w_int[k][:], w.rearrange("(n f) c -> f n c", f=P)).then_inc(loaded, 16)
            sp.dma_start(w_int[2][:], w_down.rearrange("c (n f) -> c n f", f=P)).then_inc(loaded, 16)

        @block.gpsimd
        def _(pool):
            pool.wait_ge(loaded, 48)
            for k in range(3):
                nc.gpsimd.tensor_scalar(w_f[k][:], w_int[k][:], SCALE, None, ALU.mult).then_inc(dequant, 1)

        @block.tensor
        def _(pe):
            for k in range(3):
                pe.wait_ge(dequant, k + 1)
                for n in range(NF):
                    mm = nc.tensor.transpose(core.S[k % 2][:, (512 * (k // 2)) + n * P:(512 * (k // 2)) + (n + 1) * P],
                                             w_f[k][:, n, :], core.ident[:])
                mm.then_inc(turned, 1)
            norm.tensor(pe)
            pe.wait_ge(copied, 3)

            def down(c):
                pe.wait_ge(hidden, NF * (c + 1))
                if c >= 1:
                    pe.wait_ge(added, c)
                for k in range(4):
                    for f in range(NF):
                        mm = nc.tensor.matmul(core.O[:, k * C:(k + 1) * C], h[c % 2][:, f, k * P:(k + 1) * P],
                                              w_T[2][:, f, :], start=(f == 0), stop=(f == NF - 1))
                mm.then_inc(downed, 1)

            for c in range(4):
                pe.wait_ge(norm.rounded, c + 1)
                for f in range(NF):
                    u = c * NF + f
                    x = norm.xT[:, c * 512:(c + 1) * 512]
                    if u >= 2:
                        pe.wait_ge(silued, u - 1)
                        pe.wait_ge(hidden, u - 1)
                    nc.tensor.matmul(core.S[u % 2][:, 0:512], w_T[0][:, f, :], x, start=True, stop=True)\
                        .then_inc(gated, 1)
                    nc.tensor.matmul(core.S[u % 2][:, 512:1024], w_T[1][:, f, :], x, start=True, stop=True)\
                        .then_inc(upped, 1)
                if c >= 1:
                    down(c - 1)
            down(3)

        @block.scalar
        def _(act):
            norm.scalar(act)
            for k in range(3):
                act.wait_ge(turned, k + 1)
                o = 512 * (k // 2)
                nc.scalar.activation(w_T[k][:], core.S[k % 2][:, o:o + FH].rearrange("p (n c) -> p n c", c=P),
                                     ACT.Copy).then_inc(copied, 1)
            norm.round(act)
            for u in range(4 * NF):
                act.wait_ge(gated, u + 1)
                if u >= 2:
                    act.wait_ge(hidden, u - 1)
                nc.scalar.activation(silu[u % 2][:], core.S[u % 2][:, 0:512], ACT.Silu).then_inc(silued, 1)

        @block.vector
        def _(dve):
            norm.vector(dve)

            def add(c):
                dve.wait_ge(downed, c + 1)
                x = core.x[:, 4 * c:4 * c + 4, :]
                nc.vector.tensor_tensor(x, core.O[:].rearrange("p (n c) -> p n c", c=C), x, ALU.add)\
                    .then_inc(added, 1)

            for c in range(4):
                for f in range(NF):
                    u = c * NF + f
                    dve.wait_ge(silued, u + 1)
                    dve.wait_ge(upped, u + 1)
                    if c >= 2:
                        dve.wait_ge(downed, c - 1)
                    nc.vector.tensor_tensor(h[c % 2][:, f, :], core.S[u % 2][:, 512:1024], silu[u % 2][:],
                                            ALU.mult).then_inc(hidden, 1)
                if c >= 1:
                    add(c - 1)
            add(3)


def mixture(core, gate_w, w1, b1, w2, b2):
    nc = core.nc
    with ExitStack() as ctx:
        norm = Norm(core, ctx, "moe_norm", exact=True)

        def sb(n, shape, dt=F32):
            return ctx.enter_context(nc.sbuf_tensor(f"moe_{n}", shape, dt))

        factor = sb("factor", [P, NT, E])
        any_kept = sb("any_kept", [1, 1], I32)

        with ExitStack() as c1:
            def sb1(n, shape, dt=F32):
                return c1.enter_context(nc.sbuf_tensor(f"gate_{n}", shape, dt))

            def sem(n):
                return c1.enter_context(nc.semaphore(f"gate_{n}"))

            gw, gwT = sb1("gw", [E, C]), sb1("gwT", [C, E])
            ones = sb1("ones", [P, P])
            order = sb1("order", [P, E])
            probs, left, score = (sb1(n, [P, NT, E]) for n in ("probs", "left", "score"))
            first, second = sb1("first", [P, NT, E]), sb1("second", [P, NT, E])
            most, total = sb1("most", [P, NT]), sb1("total", [P, NT])
            count, keep = sb1("count", [P, E]), sb1("keep", [P, E])
            loaded, consts, gw_turned, gw_copied = sem("loaded"), sem("consts"), sem("gw_turned"), sem("gw_copied")
            logits_done, shifted, exped = sem("logits_done"), sem("shifted"), sem("exped")
            counted, summed, dve_done = sem("counted"), sem("summed"), sem("dve_done")
            block = c1.enter_context(nc.Block())

            @block.sync
            def _(sp):
                sp.dma_start(gw[:], gate_w).then_inc(loaded, 16)

            @block.gpsimd
            def _(pool):
                nc.gpsimd.memset(ones[:], 1.0).then_inc(consts, 1)
                nc.gpsimd.iota(order[:], pattern=[[-1, E]], base=E, channel_multiplier=0,
                               allow_small_or_imprecise_dtypes=True).then_inc(consts, 1)

            @block.tensor
            def _(pe):
                pe.wait_ge(loaded, 16)
                nc.tensor.transpose(core.PJ[:, 0:E], gw[:], core.ident[0:E, 0:E]).then_inc(gw_turned, 1)

                def logits(g):
                    if g == 0:
                        pe.wait_ge(gw_copied, 1)
                    pe.wait_ge(norm.rounded, g + 1)
                    for t in range(g * LANES, (g + 1) * LANES):
                        mm = nc.tensor.matmul(core.PJ[:, t * E:(t + 1) * E], norm.xT[:, t * P:(t + 1) * P],
                                              gwT[:], start=True, stop=True)
                    return mm

                for g in range(norm.STEPS):
                    norm.tensor(pe, [g])
                    if g >= 1:
                        logits(g - 1)
                logits(norm.STEPS - 1).then_inc(logits_done, 1)
                pe.wait_ge(consts, 2)
                pe.wait_ge(counted, 1)
                nc.tensor.matmul(core.O[:, 0:E], ones[:], count[:], start=True, stop=True).then_inc(summed, 1)

            @block.scalar
            def _(act):
                norm.scalar(act)
                act.wait_ge(gw_turned, 1)
                nc.scalar.activation(gwT[:], core.PJ[:, 0:E], ACT.Copy).then_inc(gw_copied, 1)
                norm.round(act)
                act.wait_ge(shifted, 1)
                nc.scalar.activation(probs[:], left[:], ACT.Exp).then_inc(exped, 1)

            @block.vector
            def _(dve):
                norm.vector(dve)
                n = [0]

                def then(ins):
                    n[0] += 1
                    ins.then_inc(dve_done, 1)
                    dve.wait_ge(dve_done, n[0])

                def by_row(ap):
                    return ap.unsqueeze(2).broadcast_to([P, NT, E])

                def by_expert(ap):
                    return ap.unsqueeze(1).broadcast_to([P, NT, E])

                logits = core.PJ[:, 0:NT * E].rearrange("p (n e) -> p n e", e=E)
                dve.wait_ge(logits_done, 1)
                then(nc.vector.reduce_max(most[:], logits, AX.X))
                nc.vector.tensor_tensor(left[:], logits, by_row(most[:]), ALU.subtract).then_inc(shifted, 1)
                dve.wait_ge(exped, 1)
                then(nc.vector.reduce_sum(total[:], probs[:], AX.X))
                then(nc.vector.reciprocal(total[:], total[:]))
                then(nc.vector.tensor_tensor(probs[:], probs[:], by_row(total[:]), ALU.mult))
                dve.wait_ge(consts, 2)

                def top(p, out):
                    then(nc.vector.reduce_max(most[:], p[:], AX.X))
                    then(nc.vector.tensor_tensor(score[:], p[:], by_row(most[:]), ALU.is_equal))
                    then(nc.vector.tensor_tensor(score[:], score[:], by_expert(order[:]), ALU.mult))
                    then(nc.vector.reduce_max(most[:], score[:], AX.X))
                    then(nc.vector.tensor_tensor(out[:], score[:], by_row(most[:]), ALU.is_equal))

                top(probs, first)
                then(nc.vector.scalar_tensor_tensor(out=left[:], in0=first[:], scalar=-2.0, in1=probs[:],
                                                    op0=ALU.mult, op1=ALU.add))
                top(left, second)
                then(nc.vector.tensor_tensor(first[:], first[:], second[:], ALU.add))
                nc.vector.reduce_sum(count[:], first[:].rearrange("p n e -> p e n"), AX.X).then_inc(counted, 1)
                then(nc.vector.tensor_tensor(probs[:], probs[:], first[:], ALU.mult))
                dve.wait_ge(summed, 1)
                then(nc.vector.tensor_scalar(keep[:], core.O[:, 0:E], float(CAP), None, ALU.is_le))
                then(nc.vector.tensor_tensor(factor[:], probs[:], by_expert(keep[:]), ALU.mult))
                then(nc.vector.reduce_max(any_kept[:], keep[0:1, :], AX.X))

        experts(core, norm.xT, factor, any_kept, w1, b1, w2, b2)


def experts(core, xT, factor, any_kept, w1, b1, w2, b2):
    nc = core.nc
    CH = 4
    with ExitStack() as ctx:
        def sb(n, shape, dt=F32):
            return ctx.enter_context(nc.sbuf_tensor(f"exp_{n}", shape, dt))

        def sem(n):
            return ctx.enter_context(nc.semaphore(f"exp_{n}"))

        w = [sb("w1", [P, P]), sb("w2", [P, P])]
        wT = [sb("w1T", [P, P]), sb("w2T", [P, P])]
        b1_col, b2_row = sb("b1", [P, 1]), sb("b2", [1, P])
        h = [sb("h0", [P, 512]), sb("h1", [P, 512])]
        loaded, turned, copied = sem("loaded"), sem("turned"), sem("copied")
        upped, silued, downed, added = sem("upped"), sem("silued"), sem("downed"), sem("added")
        out_bank = [core.O, core.PJ]
        block = ctx.enter_context(nc.Block())

        @block.sync
        def _(sp):
            kept = sp.value_load(any_kept[0:1, 0:1], min_val=0, max_val=1)
            with sp.If(kept > 0):
                def load(e):
                    wait(sp, downed, e * CH)
                    one = bass.ds(e, 1)
                    sp.dma_start(w[0][:], w1[one, :, :].rearrange("e f c -> (e f) c")).then_inc(loaded, 16)
                    sp.dma_start(w[1][:], w2[one, :, :].rearrange("e g f -> (e g) f")).then_inc(loaded, 16)
                    sp.dma_start(b1_col[:], b1[one, :].rearrange("e f -> f e")).then_inc(loaded, 16)
                    sp.dma_start(b2_row[:], b2[one, :]).then_inc(loaded, 16)

                load(0)
                with sp.Fori(1, E) as e:
                    load(e)

        @block.tensor
        def _(pe):
            kept = pe.value_load(any_kept[0:1, 0:1], min_val=0, max_val=1)
            with pe.If(kept > 0):
                def expert(e):
                    wait(pe, loaded, (e + 1) * 64)
                    for k in range(2):
                        mm = nc.tensor.transpose(core.TP[k][:, 0:P], w[k][:], core.ident[:])
                    mm.then_inc(turned, 1)
                    wait(pe, copied, e + 1)

                    def down(c):
                        wait(pe, silued, e * CH + (c + 1))
                        wait(pe, added, e * CH + (c - 1))
                        for k in range(4):
                            out = out_bank[c % 2][:, k * P:(k + 1) * P]
                            nc.tensor.matmul(out, h[c % 2][:, k * P:(k + 1) * P], wT[1][:], start=True, stop=False)
                            mm = nc.tensor.matmul(out, core.ones_row[:], b2_row[:], start=False, stop=True)
                        mm.then_inc(downed, 1)

                    for c in range(CH):
                        wait(pe, silued, e * CH + (c - 1))
                        nc.tensor.matmul(core.S[c % 2][:, 0:512], wT[0][:], xT[:, c * 512:(c + 1) * 512],
                                         start=True, stop=True).then_inc(upped, 1)
                        if c >= 1:
                            down(c - 1)
                    down(CH - 1)

                expert(0)
                with pe.Fori(1, E) as e:
                    expert(e)

        @block.scalar
        def _(act):
            kept = act.value_load(any_kept[0:1, 0:1], min_val=0, max_val=1)
            with act.If(kept > 0):
                def expert(e):
                    wait(act, turned, e + 1)
                    wait(act, downed, e * CH)
                    for k in range(2):
                        last = nc.scalar.activation(wT[k][:], core.TP[k][:, 0:P], ACT.Copy)
                    last.then_inc(copied, 1)
                    for c in range(CH):
                        wait(act, upped, e * CH + (c + 1))
                        wait(act, downed, e * CH + (c - 1))
                        nc.scalar.activation(h[c % 2][:], core.S[c % 2][:, 0:512], ACT.Silu, bias=b1_col[:, 0:1])\
                            .then_inc(silued, 1)

                expert(0)
                with act.Fori(1, E) as e:
                    expert(e)

        @block.vector
        def _(dve):
            kept = dve.value_load(any_kept[0:1, 0:1], min_val=0, max_val=1)
            with dve.If(kept > 0):
                def expert(e):
                    for c in range(CH):
                        wait(dve, downed, e * CH + (c + 1))
                        wait(dve, added, e * CH + c)
                        for k in range(4):
                            t = 4 * c + k
                            last = nc.vector.scalar_tensor_tensor(
                                out=core.x[:, t, :], in0=out_bank[c % 2][:, k * P:(k + 1) * P],
                                scalar=factor[:, t, bass.ds(e, 1)], in1=core.x[:, t, :], op0=ALU.mult, op1=ALU.add)
                        last.then_inc(added, 1)

                expert(0)
                with dve.Fori(1, E) as e:
                    expert(e)


def store(core, out):
    nc = core.nc
    with nc.semaphore("stored") as stored, nc.Block() as block:
        @block.sync
        def _(sp):
            sp.dma_start(out.rearrange("(n p) c -> p n c", p=P), core.x[:]).then_inc(stored, 16)
            sp.wait_ge(stored, 16)


def program(nc, inputs, out):
    with ExitStack() as ctx:
        core = Core(nc, ctx)
        a = inputs
        w0 = a["L0_attn_W_qkv"]
        nq0 = 2 * KVH * D
        attention_layer(core, "a0", 2, w0[:, 0:nq0], w0[:, nq0:nq0 + KVH * D], w0[:, nq0 + KVH * D:],
                        a["L0_attn_W_out"], alibi_slopes(2 * KVH),
                        x_in=a["L0_attn_inputs"].rearrange("b s c -> (b s) c"))
        feed_forward(core, a["L0_ffn_w_gate"], a["L0_ffn_w_up"], a["L0_ffn_w_down"])
        attention_layer(core, "a1", 1, a["L1_attn_Wq"], a["L1_attn_Wk"], a["L1_attn_Wv"], a["L1_attn_Wo"],
                        None, bo=a["L1_attn_bo"])
        mixture(core, a["L1_ffn_gate_w"], a["L1_ffn_w1"], a["L1_ffn_b1"], a["L1_ffn_w2"], a["L1_ffn_b2"])
        store(core, out.rearrange("b s c -> (b s) c"))


_INS = ['L0_attn_inputs', 'L0_attn_W_qkv', 'L0_attn_W_out', 'L0_ffn_w_gate', 'L0_ffn_w_up', 'L0_ffn_w_down',
        'L1_attn_Wq', 'L1_attn_Wk', 'L1_attn_Wv', 'L1_attn_Wo', 'L1_attn_bo',
        'L1_ffn_gate_w', 'L1_ffn_w1', 'L1_ffn_b1', 'L1_ffn_w2', 'L1_ffn_b2']


def kernel(**inputs):
    import concourse.bacc as bacc
    from concourse.bass_utils import run_bass_kernel_spmd

    nc = bacc.Bacc("TRN2", target_bir_lowering=False, num_devices=1,
                   dynamic_dma_scratch_size=1024)
    arrays, aps = {}, {}
    for name in _INS:
        a = np.ascontiguousarray(inputs[name])
        arrays[name] = a
        aps[name] = nc.dram_tensor(name, a.shape, mybir.dt.from_np(a.dtype), kind="ExternalInput").ap()
    out = nc.dram_tensor("out", (BATCH, SEQ, C), F32, kind="ExternalOutput").ap()
    program(nc, aps, out)
    r = run_bass_kernel_spmd(nc, [arrays], core_ids=[0])
    return r.results[0]["out"]
```
